# Optimizing a Trainium2 kernel written in Bass

```python
import numpy as np
import jax
import jax.numpy as jnp

def _softmax(x, axis=-1):
    return jax.nn.softmax(x, axis=axis)

def _gelu(x):
    return jax.nn.gelu(x, approximate=True)

def _silu(x):
    return jax.nn.silu(x)

def _sigmoid(x):
    return jax.nn.sigmoid(x)

def _layernorm(x, axis=-1, eps=1e-05):
    m = jnp.mean(x, axis=axis, keepdims=True)
    v = jnp.var(x, axis=axis, keepdims=True)
    return (x - m) / jnp.sqrt(v + eps)

def _scatter_add(tgt, idx, src, axis=0):
    return tgt.at[idx].add(src)

def _segment_sum(src, seg, n):
    return jax.ops.segment_sum(src, seg, n)
kernel_name = 'mk_seq_preln_d1_jaxref_r4_29c9e0'

def setup_inputs(seed: int=0):
    np.random.seed(seed)
    _w = jnp.asarray

    def _L0_attn_setup():
        import jax, jax.numpy as jnp
        import numpy as np
        NUM_HEADS = 16

        def _l2_normalize_complex(z):
            n = jnp.sqrt(jnp.sum(jnp.abs(z) ** 2, axis=-1, keepdims=True))
            return z / n
        key = jax.random.key(seed)
        k1, k2, k3, k4 = jax.random.split(key, 4)
        B, S, D = (4, 1024, 512)
        scale = 1.0 / np.sqrt(D)
        return {'x': jax.random.normal(k1, (B, S, D), dtype=jnp.float32), 'W_q': jax.random.normal(k2, (D, D), dtype=jnp.float32) * scale, 'W_kv': jax.random.normal(k3, (D, D), dtype=jnp.float32) * scale, 'W_o': jax.random.normal(k4, (D, D), dtype=jnp.float32) * scale}
    _L0_attn_in = _L0_attn_setup()

    def _L0_ffn_setup():
        import jax, jax.numpy as jnp
        import numpy as np
        B, S, H, I = (1, 64, 512, 1536)

        def _quantized_matmul(x, w, scale):
            wq = w.astype(jnp.float8_e4m3fn).astype(x.dtype)
            y = jnp.einsum('bsi,io->bso', x, wq)
            return y * scale
        key = jax.random.key(seed)
        ks = jax.random.split(key, 7)
        return {'x': jax.random.normal(ks[0], (B, S, H), dtype=jnp.float32), 'gate_w': jax.random.normal(ks[1], (H, I), dtype=jnp.float32) * 0.02, 'up_w': jax.random.normal(ks[2], (H, I), dtype=jnp.float32) * 0.02, 'down_w': jax.random.normal(ks[3], (I, H), dtype=jnp.float32) * 0.02, 'gate_scale': jax.random.uniform(ks[4], (I,), dtype=jnp.float32, minval=0.5, maxval=1.5), 'up_scale': jax.random.uniform(ks[5], (I,), dtype=jnp.float32, minval=0.5, maxval=1.5), 'down_scale': jax.random.uniform(ks[6], (H,), dtype=jnp.float32, minval=0.5, maxval=1.5)}
    _L0_ffn_in = _L0_ffn_setup()
    _d = {'L0_attn_x': _L0_attn_in['x'], 'L0_attn_W_q': _L0_attn_in['W_q'], 'L0_attn_W_kv': _L0_attn_in['W_kv'], 'L0_attn_W_o': _L0_attn_in['W_o'], 'L0_ffn_gate_w': _L0_ffn_in['gate_w'], 'L0_ffn_up_w': _L0_ffn_in['up_w'], 'L0_ffn_down_w': _L0_ffn_in['down_w'], 'L0_ffn_gate_scale': _L0_ffn_in['gate_scale'], 'L0_ffn_up_scale': _L0_ffn_in['up_scale'], 'L0_ffn_down_scale': _L0_ffn_in['down_scale']}
    _x0 = _d['L0_attn_x']
    _d['L0_attn_x'] = jax.random.normal(jax.random.fold_in(jax.random.key(seed), 1), (4, 512, 512), dtype=_x0.dtype)
    del _x0
    return _d

def reference(L0_attn_x, L0_attn_W_q, L0_attn_W_kv, L0_attn_W_o, L0_ffn_gate_w, L0_ffn_up_w, L0_ffn_down_w, L0_ffn_gate_scale, L0_ffn_up_scale, L0_ffn_down_scale):

    def _L0_attn_ref(x, W_q, W_kv, W_o):
        import jax, jax.numpy as jnp
        import numpy as np
        NUM_HEADS = 16

        def _l2_normalize_complex(z):
            n = jnp.sqrt(jnp.sum(jnp.abs(z) ** 2, axis=-1, keepdims=True))
            return z / n
        B, S, D = x.shape
        H = NUM_HEADS
        hd = D // H
        q = (x @ W_q.T).reshape(B, S, H, hd)
        kv = (x @ W_kv.T).reshape(B, S, H, hd)
        qf = jnp.fft.fft(q, axis=-1)
        kvf = jnp.fft.fft(kv, axis=-1)
        qf = _l2_normalize_complex(qf)
        kvf = _l2_normalize_complex(kvf)
        kvf = jnp.cumsum(kvf, axis=1)
        qv = qf * kvf
        values_hat = jnp.fft.ifft(qv, axis=-1).real.astype(x.dtype)
        values_hat = values_hat.reshape(B, S, D)
        return values_hat @ W_o.T

    def _L0_ffn_ref(x, gate_w, up_w, down_w, gate_scale, up_scale, down_scale):
        import jax, jax.numpy as jnp
        import numpy as np
        B, S, H, I = (1, 64, 512, 1536)

        def _quantized_matmul(x, w, scale):
            wq = w.astype(jnp.float8_e4m3fn).astype(x.dtype)
            y = jnp.einsum('bsi,io->bso', x, wq)
            return y * scale
        gate = jax.nn.silu(_quantized_matmul(x, gate_w, gate_scale))
        up = _quantized_matmul(x, up_w, up_scale)
        fuse = gate * up
        return _quantized_matmul(fuse, down_w, down_scale)
    x = L0_attn_x
    x = x + _L0_attn_ref(_layernorm(x, axis=-1), L0_attn_W_q, L0_attn_W_kv, L0_attn_W_o)
    x = x + _L0_ffn_ref(_layernorm(x, axis=-1), L0_ffn_gate_w, L0_ffn_up_w, L0_ffn_down_w, L0_ffn_gate_scale, L0_ffn_up_scale, L0_ffn_down_scale)
    return x

_drawn_inputs = setup_inputs


def setup_inputs(seed=0):
    import zlib

    import numpy as np

    out = dict(_drawn_inputs(seed))
    spreads = {}
    factors = {}
    for name, (base, spread) in spreads.items():
        noise = np.random.default_rng([zlib.crc32(name.encode()), seed]).standard_normal(out[name].shape)
        drawn = base * np.exp(spread * noise) if base else spread * noise
        out[name] = jnp.asarray(drawn.astype(out[name].dtype))
    for name, factor in factors.items():
        out[name] = (out[name] * factor).astype(out[name].dtype)
    return out
```

```python
import numpy as np
import concourse.bass as bass
from concourse import mybir
from contextlib import ExitStack

F32 = mybir.dt.float32
F32R = mybir.dt.float32r
F16 = mybir.dt.float16
BF16 = mybir.dt.bfloat16
U16 = mybir.dt.uint16
ALU = mybir.AluOpType
ACT = mybir.ActivationFunctionType
AX = mybir.AxisListType

P = 128
NB = 4
NT = 4
KT = 4
D = 512
NI = 12
NH = 16
HD = 32
EPS = 1e-5


def constants():
    n = np.arange(HD)[:, None]
    j = np.arange(16)[None, :]
    ang = 2.0 * np.pi * n * j / HD
    alt = np.where(n[:, 0] % 2 == 0, 1.0, -1.0)
    fre, fim = np.sqrt(2.0) * np.cos(ang), -np.sqrt(2.0) * np.sin(ang)
    fre[:, 0], fim[:, 0] = 1.0, alt
    ire, iim = np.cos(ang) / HD, -np.sin(ang) / HD
    ire[:, 0], iim[:, 0] = 1.0 / HD, alt / HD
    fwd = np.zeros((P, 2, 64))
    inv = np.zeros((P, 2, 2, P))
    for h in range(4):
        r = slice(HD * h, HD * h + HD)
        fwd[r, 0, 16 * h:16 * h + 16] = fre
        fwd[r, 1, 16 * h:16 * h + 16] = fim
        for par in range(2):
            c = 16 * (4 * par + h)
            inv[r, par, 0, c:c + 16] = ire
            inv[r, par, 1, c:c + 16] = iim
    ident = np.eye(P)
    tri = np.triu(np.ones((P, P)))
    ones = np.ones((P, P))
    return (np.concatenate([fwd.reshape(P, -1), ident], 1).astype(np.float32),
            np.concatenate([inv.reshape(P, -1), tri, ones], 1).astype(np.float32))


class Line:

    def __init__(self, sem):
        self.sem, self.n, self.q = sem, 0, []

    def do(self, fn, *after, mark=True):
        self.q.append((fn, after, mark))
        if mark:
            self.n += 1
        return (self.sem, self.n)

    def run(self, eng):
        for fn, after, mark in self.q:
            for sem, value in after:
                eng.wait_ge(sem, value)
            ins = fn(eng)
            if mark:
                ins.then_inc(self.sem, 1)


def build(nc, x, xT, w_q, w_kv, woT, gate_w, up_w, down_w, gs_d, us_d, ds_d, cst_d, cst2_d, out):
    ctx = ExitStack()
    with ctx:
        def sb(name, shape, dt):
            return ctx.enter_context(nc.sbuf_tensor(name, shape, dt))

        def sem(name):
            return ctx.enter_context(nc.semaphore(name))

        cst = sb("cst", [P, 256], F32)
        gu = sb("gu", [P, 3, 8, 512], F16)
        dw = sb("dw", [P, NI, 512], F32R)
        wf = sb("wf", [P, 2, 2, KT, 512], F32R)
        wo = sb("wo", [P, 2, KT, 512], F32R)
        xTr = sb("xTr", [P, 2, 512], F32)
        xTs = sb("xTs", [P, 2, KT, 512], F32R)
        qk = sb("qk", [P, NT, 2, 512], F32)
        ks = sb("ks", [P, 2, NT, 512], F16)
        tu = sb("tu", [P, 2, 512], F32)
        pT = sb("pT", [P, 2, 512], F32R)
        h = sb("h", [P, 2, NT, 512], F32)
        hT = sb("hT", [P, 2, 2, KT, 512], F16)
        fu = sb("fu", [P, 2, 2, 512], F32R)
        sl = sb("sl", [P, 2, 512], F32)
        ff = sb("ff", [P, 2, 512], F32)
        ds = sb("ds", [P, 512], F32)
        gs = sb("gs", [P, NI], F32)
        us = sb("us", [P, NI], F32)
        tr16 = sb("tr16", [P, 2, P], F16)
        mq = sb("mq", [P, 2, 512], BF16)
        bst = sb("bst", [P, 8, 6], F32)
        mv1 = sb("mv1", [P, NT, 2], F32)
        mv2 = sb("mv2", [P, NT, 2], F32)
        S = sb("S", [P, NT, 32], F32)
        E = sb("E", [P, 132], F32)
        Q = sb("Q", [P, 132], F32)
        y0 = sb("y0", [P, 132], F32)
        ya = sb("ya", [P, 132], F32)
        yy = sb("yy", [P, 132], F32)
        rv = sb("rv", [P, NT], F32)
        sc = sb("sc", [P, NT, 32], F32)
        E2 = sb("E2", [P, 5, NT], F32)
        wst = sb("wst", [P, 8, 6], F32)
        wmv = sb("wmv", [P, 8, 2], F32)

        fwd = cst[:, 0:128].rearrange("p (a c) -> p a c", a=2)
        ident = cst[:, 128:256]
        cst2 = sl[:, :, :].rearrange("p a n -> p (a n)")[:, 0:768]
        inv = cst2[:, 0:512].rearrange("p (a c) -> p a c", a=4)
        stage = hT[:, 1, :, :, :].rearrange("p a k n -> p (a k n)").bitcast(F32).rearrange("p (s n) -> p s n", s=4)
        raw = [hT[:, 0, :, :, :].rearrange("p a k n -> p (a k n)").bitcast(F32).rearrange("p (s n) -> p s n", s=4),
               gu[:, 1, :, :].rearrange("p k n -> p (k n)").bitcast(F32).rearrange("p (s n) -> p s n", s=4)]
        woR = gu[:, 2, :, :].rearrange("p k n -> p (k n)").bitcast(F32).rearrange("p (s n) -> p s n", s=4)

        def bank(name):
            return ctx.enter_context(nc.psum_tensor(name, [P, 512], F32))

        bd = [bank(f"bd{i}") for i in range(NT)]
        bg, bu = bank("bg"), bank("bu")
        ba = [bank("ba0"), bank("ba1")]

        pe, act, dve, pool = (Line(sem(n)) for n in ("s_pe", "s_act", "s_dve", "s_pool"))
        sp = Line(sem("s_sp"))

        sent = {}

        def dma(dst, src, name, *after):
            if name not in sent:
                sent[name] = [sem("d_" + name), 0]
            s = sent[name]
            s[1] += 16
            sp.do(lambda e: e.dma_start(dst, src).then_inc(s[0], 16), *after, mark=False)
            return (s[0], s[1])

        a_free = [[], []]
        a_next = [0]

        def a_bank():
            i = a_next[0] % 2
            a_next[0] += 1
            return i

        xtr_free = [[], []]
        xts_read = []
        t_xts = {}

        t_xtr = {}

        def load_xT(b, k):
            slot = k % 2
            t_xtr[b, k] = dma(xTr[:, slot, :], xT[P * k:P * k + P, D * b:D * b + D], f"xtr{slot}", *xtr_free[slot])

        def split_xT(b, k, lo_on=None):
            lo_on = lo_on or pool
            slot = k % 2
            hi = act.do(lambda e: e.activation(xTs[:, 0, k, :], xTr[:, slot, :], ACT.Copy), t_xtr[b, k], *xts_read)
            lo = lo_on.do(lambda e: e.tensor_tensor(xTs[:, 1, k, :], xTr[:, slot, :],
                                                    xTs[:, 0, k, :].bitcast(F32), ALU.subtract), hi)
            xtr_free[slot] = [hi, lo]
            t_xts[b, k] = lo

        t_x = {}
        h_free = [[], []]
        t_mv1 = {}
        mv1_read = []

        def load_x(b):
            for t in range(NT):
                after = h_free[b % 2][t] if h_free[b % 2] else ()
                t_x[b, t] = dma(h[:, b % 2, t, :], x[D * b + P * t:D * b + P * t + P, :], f"x{b % 2}{t}", *after)

        def stats1(b, t):
            st = dve.do(lambda e: e.bn_stats(bst[:, t, :], h[:, b % 2, t, :]), t_x[b, t])
            t_mv1[b, t] = dve.do(lambda e: e.bn_aggr(mv1[:, t, :], bst[:, t, :]), st)

        qk_free = {}
        t_S = {}
        t_qk = {}
        sq_free = []

        def qk_piece(b, t):
            nonlocal sq_free
            done = []
            sqs = []
            for w in range(2):
                i = a_bank()
                first = True
                for k in range(KT):
                    for part_x, part_w in ((0, 0), (0, 1), (1, 0)):
                        last = k == KT - 1 and part_x == 1
                        pe_t = pe.do(lambda e, w=w, k=k, part_x=part_x, part_w=part_w, first=first, last=last, i=i: e.matmul(
                            ba[i][:, :], xTs[:, part_x, k, P * t:P * t + P], wf[:, w, part_w, k, :],
                            start=first, stop=last),
                            *(([*a_free[i]] + [t_xts[b, kk] for kk in range(KT)] + t_wf[w]) if first else []), mark=last)
                        first = False
                sq = act.do(lambda e, i=i, w=w: e.activation(tu[:, w, :], ba[i][:, :], ACT.Square), pe_t, *sq_free)
                cp = act.do(lambda e, i=i, w=w: e.activation(qk[:, t, w, :], ba[i][:, :], ACT.Copy),
                            *qk_free.get((t, w), []))
                a_free[i] = [cp]
                sqs.append(sq)
                done.append(cp)
            if t == NT - 1:
                xts_read[:] = [pe_t]
            for w in range(2):
                v = tu[:, w, :].rearrange("p (a c j) -> p c a j", a=2, c=NH)
                red = dve.do(lambda e, w=w, v=v: e.tensor_reduce(S[:, t, NH * w:NH * w + NH], v, AX.XY, ALU.add), sqs[w])
            sq_free = [red]
            t_S[b, t] = red
            t_qk[b, t] = done

        def refined_rsqrt(e_ap, q_ap, y_ap, a_ap, out_ap, ready, q_read):
            sq = act.do(lambda e: e.activation(q_ap, e_ap, ACT.Sqrt), ready, *q_read)
            r = dve.do(lambda e: e.reciprocal(y_ap, q_ap), sq)
            a = dve.do(lambda e: e.scalar_tensor_tensor(out=a_ap, in0=y_ap, scalar=-0.5, in1=y_ap,
                                                        op0=ALU.mult, op1=ALU.mult), r)
            b = dve.do(lambda e: e.tensor_tensor(a_ap, a_ap, e_ap, ALU.mult), a)
            return dve.do(lambda e: e.scalar_tensor_tensor(out=out_ap, in0=a_ap, scalar=1.5, in1=y_ap,
                                                           op0=ALU.add, op1=ALU.mult), b)

        t_sc = {}

        def norm_piece(b):
            ve = dve.do(lambda e: e.tensor_scalar(E[:, 0:NT], mv1[:, :, 1], EPS, None, ALU.add),
                        *[t_mv1[b, t] for t in range(NT)])
            r = dve.do(lambda e: e.reciprocal(rv[:, :], E[:, 0:NT]), ve)
            ss = dve.do(lambda e: e.tensor_tensor(E[:, NT:132].rearrange("p (t c) -> p t c", t=NT), S[:, :, :],
                                                  rv[:, :].unsqueeze(2).broadcast_to([P, NT, 32]), ALU.mult), r, t_S[b, NT - 1])
            y = refined_rsqrt(E[:, :], Q[:, :], y0[:, :], ya[:, :], yy[:, :], ss, [])
            t_sc[b] = dve.do(lambda e: e.tensor_tensor(sc[:, :, :], yy[:, NT:132].rearrange("p (t c) -> p t c", t=NT),
                                                       yy[:, 0:NT].unsqueeze(2).broadcast_to([P, NT, 32]), ALU.mult), y)

        t_qn = {}
        t_ks = {}
        ks_free = {}

        def head_scale(t, w):
            return sc[:, t, NH * w:NH * w + NH].unsqueeze(1).unsqueeze(3).broadcast_to([P, 2, NH, 16])

        def split_heads(ap):
            return ap.rearrange("p (a c j) -> p a c j", a=2, c=NH)

        def scale_piece(b, t):
            kn = dve.do(lambda e: e.tensor_tensor(split_heads(qk[:, t, 1, :]), split_heads(qk[:, t, 1, :]),
                                                  head_scale(t, 1), ALU.mult), t_sc[b], t_qk[b, t][1])
            hi = act.do(lambda e: e.activation(ks[:, 0, t, :], qk[:, t, 1, :], ACT.Copy), kn, *ks_free.get(t, []))
            lo = pool.do(lambda e: e.tensor_tensor(ks[:, 1, t, :], qk[:, t, 1, :], ks[:, 0, t, :], ALU.subtract), hi)
            t_qn[b, t] = dve.do(lambda e: e.tensor_tensor(split_heads(qk[:, t, 0, :]), split_heads(qk[:, t, 0, :]),
                                                          head_scale(t, 0), ALU.mult), t_qk[b, t][0])
            t_ks[b, t] = lo

        t_p = {}
        tu_free = [[]]

        def tri_piece(b, t):
            nonlocal sq_free
            i = a_bank()
            for s in range(t + 1):
                for part in range(2):
                    first, last = s == 0 and part == 0, s == t and part == 1
                    c = pe.do(lambda e, s=s, part=part, first=first, last=last: e.matmul(
                        ba[i][:, :], tr16[:, 0 if s == t else 1, :], ks[:, part, s, :], start=first, stop=last),
                        *(([*a_free[i]] + [t_ks[b, t], t_tr16]) if first else []), mark=last)
            if t == NT - 1:
                for s in range(NT):
                    ks_free[s] = [c]
            qn = qk[:, t, 0, :]
            T, U = tu[:, 0, :], tu[:, 1, :]
            tt = dve.do(lambda e: e.tensor_tensor(T, qn, ba[i][:, :], ALU.mult), c, t_qn[b, t], *tu_free[0])
            dve.do(lambda e: e.tensor_tensor(U[:, 0:256], qn[:, 0:256], ba[i][:, 256:512], ALU.mult))
            u = dve.do(lambda e: e.tensor_tensor(U[:, 256:512], qn[:, 256:512], ba[i][:, 0:256], ALU.mult))
            a_free[i] = [u]
            r = pool.do(lambda e: e.tensor_tensor(qn[:, 0:256], T[:, 0:256], T[:, 256:512], ALU.subtract), u)
            m = pool.do(lambda e: e.tensor_tensor(qn[:, 256:512], U[:, 0:256], U[:, 256:512], ALU.add))
            z = pool.do(lambda e: e.tensor_copy(split_heads(qn)[:, :, :, 0], split_heads(T)[:, :, :, 0]), r, m)
            tu_free[0] = [z]
            sq_free = [z]
            t_p[b, t] = z

        pT_free = [[]]
        t_pT = {}

        def pt_piece(b, t):
            i = a_bank()
            for j in range(KT):
                tp = pe.do(lambda e, j=j: e.transpose(ba[i][:, P * j:P * j + P], qk[:, t, 0, P * j:P * j + P], ident),
                           *([*a_free[i], t_p[b, t]] if j == 0 else []), mark=j == KT - 1)
            qk_free[t, 0] = [tp]
            hi = act.do(lambda e: e.activation(pT[:, 0, :], ba[i][:, :], ACT.Copy), tp, *pT_free[0])
            lo = dve.do(lambda e: e.tensor_tensor(pT[:, 1, :], ba[i][:, :], pT[:, 0, :].bitcast(F32), ALU.subtract), hi)
            a_free[i] = [lo]
            t_pT[b, t] = lo

        t_h = {}
        t_mv2 = {}

        def o_piece(b, t):
            i = a_bank()
            first = True
            for j in range(KT):
                for part_p, part_w in ((0, 0), (0, 1), (1, 0)):
                    last = j == KT - 1 and part_p == 1
                    o = pe.do(lambda e, j=j, part_p=part_p, part_w=part_w, first=first, last=last: e.matmul(
                        ba[i][:, :], pT[:, part_p, P * j:P * j + P], wo[:, part_w, j, :], start=first, stop=last),
                        *(([*a_free[i], t_pT[b, t]] + t_wo) if first else []), mark=last)
                    first = False
            pT_free[0] = [o]
            hh = h[:, b % 2, t, :]
            t_h[b, t] = dve.do(lambda e: e.tensor_tensor(hh, ba[i][:, :], hh, ALU.add), o, t_x[b, t])
            a_free[i] = [t_h[b, t]]
            st = dve.do(lambda e: e.bn_stats(bst[:, 4 + t, :], hh), t_h[b, t])
            t_mv2[b, t] = dve.do(lambda e: e.bn_aggr(mv2[:, t, :], bst[:, 4 + t, :]), st)

        t_r2 = {}

        def ln2_piece(b):
            ve = dve.do(lambda e: e.tensor_scalar(E2[:, 0, :], mv2[:, :, 1], EPS, None, ALU.add),
                        *[t_mv2[b, t] for t in range(NT)])
            t_r2[b] = refined_rsqrt(E2[:, 0, :], E2[:, 1, :], E2[:, 2, :], E2[:, 3, :], E2[:, 4, :], ve, [])

        t_hT = {}
        hT_free = [[], []]

        def ht_piece(b, t):
            hn = qk[:, t, 1, :]
            nr = dve.do(lambda e: e.tensor_scalar(hn, h[:, b % 2, t, :], mv2[:, t, 0:1], E2[:, 4, t:t + 1],
                                                  ALU.subtract, ALU.mult), t_r2[b], t_ks[b, t])
            i = a_bank()
            for k in range(KT):
                tp = pe.do(lambda e, k=k: e.transpose(ba[i][:, P * k:P * k + P], qk[:, t, 1, P * k:P * k + P], ident),
                           *([*a_free[i], nr] if k == 0 else []), mark=k == KT - 1)
            qk_free[t, 1] = [tp]
            src = ba[i][:, :].rearrange("p (k n) -> p k n", k=KT)
            hi_ap = hT[:, b % 2, 0, :, P * t:P * t + P]
            lo_ap = hT[:, b % 2, 1, :, P * t:P * t + P]
            hi = act.do(lambda e: e.activation(hi_ap, src, ACT.Copy), tp, *hT_free[b % 2])
            lo = dve.do(lambda e: e.tensor_tensor(lo_ap, src, hi_ap, ALU.subtract), hi)
            a_free[i] = [lo]
            t_hT[b, t] = lo

        t_silu = {}
        t_f = {}
        ff_free = [[], []]
        ff_next = [0]
        g_free, u_free = [], []
        fu_free = [[], []]
        t_fu = {}

        def gu_piece(b, i):
            nonlocal g_free, u_free
            c, col = i // 4, P * (i % 4)
            n = b * NI + i
            for w, bk, free in ((0, bg, g_free), (1, bu, u_free)):
                for k in range(KT):
                    for part in range(2):
                        first, last = k == 0 and part == 0, k == KT - 1 and part == 1
                        m = pe.do(lambda e, w=w, bk=bk, k=k, part=part, first=first, last=last: e.matmul(
                            bk[:, :], gu[:, c, 4 * w + k, col:col + P], hT[:, b % 2, part, k, :], start=first, stop=last),
                            *((free + [t_hT[b, t] for t in range(NT)] + t_gu[c]) if first else []), mark=last)
                if w == 0:
                    tg = m
                else:
                    tu_ = m
            if i == NI - 1:
                hT_free[b % 2] = [tu_]
            s = sl[:, n % 2, :]
            r = ff_next[0] % 2
            ff_next[0] += 1
            f = ff[:, r, :]
            si = act.do(lambda e: e.activation(s, bg[:, :], ACT.Silu, scale=gs[:, i:i + 1]), tg, t_sc_load,
                        *([t_f[n - 2]] if n >= 2 else wo_raw_read))
            g_free = [si]
            t_f[n] = dve.do(lambda e: e.scalar_tensor_tensor(out=f, in0=bu[:, :], scalar=us[:, i:i + 1], in1=s,
                                                             op0=ALU.mult, op1=ALU.mult), tu_, si, *ff_free[r])
            u_free = [t_f[n]]
            hi = act.do(lambda e: e.activation(fu[:, n % 2, 0, :], f, ACT.Copy), t_f[n], *fu_free[n % 2])
            lo = dve.do(lambda e: e.tensor_tensor(fu[:, n % 2, 1, :], f, fu[:, n % 2, 0, :].bitcast(F32), ALU.subtract), hi)
            ff_free[r] = [hi, lo]
            t_fu[n] = lo

        d_free = [[] for _ in range(NT)]
        t_d = {}

        def d_piece(b, i):
            n = b * NI + i
            for t in range(NT):
                for part in range(2):
                    t_d[t] = pe.do(lambda e, t=t, part=part: e.matmul(
                        bd[t][:, :], fu[:, n % 2, part, P * t:P * t + P], dw[:, i, :],
                        start=i == 0 and part == 0, stop=i == NI - 1 and part == 1),
                        *((([t_fu[n]] + t_dw[i]) if t == 0 else []) + (d_free[t] if i == 0 else []) if part == 0 else []),
                        mark=part == 1)
            fu_free[n % 2] = [t_d[NT - 1]]

        def fin_piece(b):
            freed = []
            for t in range(NT):
                r = ff_next[0] % 2
                ff_next[0] += 1
                y = ff[:, r, :]
                hh = h[:, b % 2, t, :]
                m = dve.do(lambda e, t=t, y=y: e.tensor_tensor(y, bd[t][:, :], ds[:, :], ALU.mult), t_d[t], t_sc_load, *ff_free[r])
                d_free[t] = [m]
                on = dve if b == NB - 1 else pool
                a = on.do(lambda e, y=y, hh=hh: e.tensor_tensor(hh, y, hh, ALU.add), m)
                ff_free[r] = [a]
                freed.append([dma(out[D * b + P * t:D * b + P * t + P, :], hh, f"o{b % 2}{t}", a)])
            h_free[b % 2] = freed

        chunks = []
        for c in range(3):
            for w, src in ((0, gate_w), (1, up_w)):
                for k in range(KT):
                    chunks.append((src[P * k:P * k + P, 512 * c:512 * c + 512], gu[:, c, 4 * w + k, :], c, None))
            for i in range(4 * c, 4 * c + 4):
                chunks.append((down_w[P * i:P * i + P, :], dw[:, i, :], c, i))
        t_gu = {c: [] for c in range(3)}
        t_dw = {}
        st_free = [[] for _ in range(4)]
        t_st = {}
        mq_free = [[], []]

        def load_chunk(n):
            t_st[n] = dma(stage[:, n % 4, :], chunks[n][0], f"st{n % 4}", *st_free[n % 4])

        def quant(n, on):
            _, dst, c, i = chunks[n]
            w = stage[:, n % 4, :]
            m = mq[:, n % 2, :]
            top = w.bitcast(U16).rearrange("p (n t) -> p n t", t=2)[:, :, 1]
            e1 = dve.do(lambda e: e.tensor_scalar(m.bitcast(U16), top, 0x7F80, 0x0040, ALU.bitwise_and, ALU.bitwise_or),
                        t_st[n], *mq_free[n % 2])
            e2 = dve.do(lambda e: e.tensor_scalar(m, m, 1.5 * 2.0 ** -6, 2.0 ** 20, ALU.max, ALU.mult), e1)
            after = wo_raw_read if (i is None and c == 2) else raw_read[1] if (i is None and c == 1) else []
            a = on.do(lambda e: e.tensor_tensor(w, w, m, ALU.add), e2)
            b = on.do(lambda e: e.tensor_tensor(dst, w, m, ALU.subtract), a, *after)
            mq_free[n % 2] = [b]
            st_free[n % 4] = [b]
            if i is None:
                t_gu[c].append(b)
            else:
                t_dw[i] = [b]
            if n + 4 < len(chunks):
                load_chunk(n + 4)

        t_cst = dma(cst[:, :], cst_d, "cst")
        t_cst2 = dma(cst2, cst2_d, "cst2")
        t_raw = {}
        for w, src in ((0, w_q), (1, w_kv)):
            for f in range(KT):
                t_raw[w, f] = dma(raw[w][:, f, :], src[P * f:P * f + P, :], f"raw{w}{f}")
            if w == 0:
                load_xT(0, 0)
                load_xT(0, 1)
        load_x(0)
        t_woR = dma(woR, woT.rearrange("(f p) n -> p f n", p=P), "woR")
        for n in range(4):
            load_chunk(n)
        dma(gs[:, :], gs_d, "sc")
        dma(us[:, :], us_d, "sc")
        t_sc_load = dma(ds[:, :], ds_d.rearrange("(a n) -> a n", a=1).broadcast_to([P, D]), "sc")

        t_tr16 = act.do(lambda e: e.activation(tr16[:, :, :], cst2[:, 512:768].rearrange("p (a n) -> p a n", a=2), ACT.Copy),
                        t_cst2)

        t_wf = [[], []]
        raw_read = [[], []]
        wo_raw_read = []

        def center(w, f):
            j = KT * w + f
            st = dve.do(lambda e: e.bn_stats(wst[:, j, :], raw[w][:, f, :]), t_raw[w, f])
            ag = dve.do(lambda e: e.bn_aggr(wmv[:, j, :], wst[:, j, :]), st)
            return dve.do(lambda e: e.tensor_scalar(raw[w][:, f, :], raw[w][:, f, :], wmv[:, j, 0:1], None, ALU.subtract), ag)

        def transform(w):
            t_c = [center(w, f) for f in range(KT)]
            for k in range(KT):
                i = a_bank()
                view = ba[i][:, :].rearrange("p (a n) -> p a n", a=2)
                for f in range(KT):
                    m = pe.do(lambda e, f=f, view=view, k=k: e.matmul(view[:, :, 64 * f:64 * f + 64], raw[w][:, f, P * k:P * k + P],
                                                                     fwd, start=True, stop=True),
                              *(a_free[i] + [t_cst] if f == 0 else []), *([t_c[f]] if k == 0 else []), mark=f == KT - 1)
                hi = act.do(lambda e, i=i, k=k: e.activation(wf[:, w, 0, k, :], ba[i][:, :], ACT.Copy), m)
                lo = dve.do(lambda e, i=i, k=k: e.tensor_tensor(wf[:, w, 1, k, :], ba[i][:, :],
                                                                wf[:, w, 0, k, :].bitcast(F32), ALU.subtract), hi)
                a_free[i] = [lo]
                t_wf[w] = [lo]
                raw_read[w] = [m]

        t_wo = []

        def transform_o():
            for j in range(KT):
                part, half = j // 2, j % 2
                i = a_bank()
                for par in range(2):
                    m = pe.do(lambda e, i=i, par=par, part=part, half=half: e.matmul(
                        ba[i][:, :], inv[:, 2 * par + part, :], woR[:, 2 * half + par, :], start=par == 0, stop=par == 1),
                        *(a_free[i] + [t_woR, t_cst2] if par == 0 else []), mark=par == 1)
                hi = act.do(lambda e, i=i, j=j: e.activation(wo[:, 0, j, :], ba[i][:, :], ACT.Copy), m)
                lo = dve.do(lambda e, i=i, j=j: e.tensor_tensor(wo[:, 1, j, :], ba[i][:, :],
                                                                wo[:, 0, j, :].bitcast(F32), ALU.subtract), hi)
                a_free[i] = [lo]
                t_wo[:] = [lo]
                wo_raw_read[:] = [m]

        transform(0)
        transform(1)
        for k in range(KT):
            split_xT(0, k, dve)
            if k + 2 < KT:
                load_xT(0, k + 2)
        hT_free[0] = raw_read[0]
        for t in range(NT):
            qk_piece(0, t)
            stats1(0, t)
            quant(t, pool)
        norm_piece(0)
        transform_o()
        for t in range(NT):
            scale_piece(0, t)
        for n in range(4, 6):
            quant(n, pool)
        for t in range(NT):
            tri_piece(0, t)
            pt_piece(0, t)
            o_piece(0, t)
        for n in range(6, 8):
            quant(n, pool)
        ln2_piece(0)
        for t in range(NT):
            ht_piece(0, t)
        for n in range(8, 12):
            quant(n, pool)
        quant_next = 12

        load_x(1)
        for k in range(2):
            load_xT(1, k)
        for k in range(KT):
            split_xT(1, k)
            if k + 2 < KT:
                load_xT(1, k + 2)

        def pieces(b, slot):
            if slot < 4:
                qk_piece(b, slot)
                if slot >= 2:
                    stats1(b, 2 * slot - 4)
                    stats1(b, 2 * slot - 3)
            if slot == 3:
                norm_piece(b)
                for t in range(NT):
                    scale_piece(b, t)
            if 5 <= slot <= 8:
                tri_piece(b, slot - 5)
            if 6 <= slot <= 9:
                pt_piece(b, slot - 6)
                o_piece(b, slot - 6)
            if slot == 9:
                ln2_piece(b)
            if slot >= 10:
                ht_piece(b, 2 * slot - 20)
                ht_piece(b, 2 * slot - 19)

        for b in range(NB):
            for i in range(NI):
                gu_piece(b, i)
                if b + 1 < NB:
                    pieces(b + 1, i)
                if (b, i) != (0, 0):
                    d_piece(*divmod(b * NI + i - 1, NI))
                if i == 0 and b > 0:
                    fin_piece(b - 1)
                    if b + 1 < NB:
                        load_x(b + 1)
                if b + 2 < NB:
                    if i == 4:
                        load_xT(b + 2, 0)
                        load_xT(b + 2, 1)
                    if 6 <= i < 10:
                        split_xT(b + 2, i - 6)
                        if i < 8:
                            load_xT(b + 2, i - 4)
                if b == 0 and i < 8:
                    for _ in range(3):
                        quant(quant_next, pool if quant_next % 2 else dve)
                        quant_next += 1
        d_piece(NB - 1, NI - 1)
        fin_piece(NB - 1)
        for name, s in sent.items():
            if name[0] == "o":
                sp.do(lambda e: e.nop(), (s[0], s[1]), mark=False)

        with nc.Block() as block:
            @block.sync
            def _(e):
                sp.run(e)

            @block.tensor
            def _(e):
                pe.run(e)

            @block.scalar
            def _(e):
                act.run(e)

            @block.vector
            def _(e):
                dve.run(e)

            @block.gpsimd
            def _(e):
                pool.run(e)


def kernel(L0_attn_x, L0_attn_W_q, L0_attn_W_kv, L0_attn_W_o, L0_ffn_gate_w, L0_ffn_up_w, L0_ffn_down_w,
           L0_ffn_gate_scale, L0_ffn_up_scale, L0_ffn_down_scale):
    import concourse.bacc as bacc
    from concourse.bass_utils import run_bass_kernel_spmd

    x = np.ascontiguousarray(np.asarray(L0_attn_x).reshape(NB * D, D))
    cst, cst2 = constants()
    arrays = {
        "x": x,
        "xT": np.ascontiguousarray(x.T),
        "w_q": np.ascontiguousarray(L0_attn_W_q),
        "w_kv": np.ascontiguousarray(L0_attn_W_kv),
        "woT": np.ascontiguousarray(np.asarray(L0_attn_W_o).T),
        "gate_w": np.ascontiguousarray(L0_ffn_gate_w),
        "up_w": np.ascontiguousarray(L0_ffn_up_w),
        "down_w": np.ascontiguousarray(L0_ffn_down_w),
        "gs": np.ascontiguousarray(np.asarray(L0_ffn_gate_scale).reshape(NI, P).T),
        "us": np.ascontiguousarray(np.asarray(L0_ffn_up_scale).reshape(NI, P).T),
        "ds": np.ascontiguousarray(L0_ffn_down_scale),
        "cst": cst,
        "cst2": cst2,
    }
    nc = bacc.Bacc("TRN2", target_bir_lowering=False, num_devices=1)
    args = [nc.dram_tensor(n + "_dram", a.shape, mybir.dt.from_np(a.dtype), kind="ExternalInput").ap()
            for n, a in arrays.items()]
    out = nc.dram_tensor("out_dram", (NB * D, D), F32, kind="ExternalOutput").ap()
    build(nc, *args, out)
    r = run_bass_kernel_spmd(nc, [{n + "_dram": a for n, a in arrays.items()}], core_ids=[0])
    return r.results[0]["out_dram"].reshape(NB, D, D)
```

```python
import numpy as np
import concourse.bass as bass
from concourse import mybir
from contextlib import ExitStack

F32 = mybir.dt.float32
F32R = mybir.dt.float32r
F16 = mybir.dt.float16
BF16 = mybir.dt.bfloat16
U16 = mybir.dt.uint16
ALU = mybir.AluOpType
ACT = mybir.ActivationFunctionType
AX = mybir.AxisListType

P = 128
NB = 4
NT = 4
KT = 4
D = 512
NI = 12
NH = 16
HD = 32
EPS = 1e-5


def constants():
    n = np.arange(HD)[:, None]
    j = np.arange(16)[None, :]
    ang = 2.0 * np.pi * n * j / HD
    alt = np.where(n[:, 0] % 2 == 0, 1.0, -1.0)
    fre, fim = np.sqrt(2.0) * np.cos(ang), -np.sqrt(2.0) * np.sin(ang)
    fre[:, 0], fim[:, 0] = 1.0, alt
    ire, iim = np.cos(ang) / HD, -np.sin(ang) / HD
    ire[:, 0], iim[:, 0] = 1.0 / HD, alt / HD
    fwd = np.zeros((P, 2, 64))
    inv = np.zeros((P, 2, 2, P))
    for h in range(4):
        r = slice(HD * h, HD * h + HD)
        fwd[r, 0, 16 * h:16 * h + 16] = fre
        fwd[r, 1, 16 * h:16 * h + 16] = fim
        for par in range(2):
            c = 16 * (4 * par + h)
            inv[r, par, 0, c:c + 16] = ire
            inv[r, par, 1, c:c + 16] = iim
    ident = np.eye(P)
    tri = np.triu(np.ones((P, P)))
    ones = np.ones((P, P))
    return (np.concatenate([fwd.reshape(P, -1), ident], 1).astype(np.float32),
            np.concatenate([inv.reshape(P, -1), tri, ones], 1).astype(np.float32))


class Line:

    def __init__(self, sem):
        self.sem, self.n, self.q = sem, 0, []

    def do(self, fn, *after, mark=True):
        self.q.append((fn, after, mark))
        if mark:
            self.n += 1
        return (self.sem, self.n)

    def run(self, eng):
        for fn, after, mark in self.q:
            for sem, value in after:
                eng.wait_ge(sem, value)
            ins = fn(eng)
            if mark:
                ins.then_inc(self.sem, 1)


def build(nc, x, xT, w_q, w_kv, woT, gate_w, up_w, down_w, gs_d, us_d, ds_d, cst_d, cst2_d, out):
    ctx = ExitStack()
    with ctx:
        def sb(name, shape, dt):
            return ctx.enter_context(nc.sbuf_tensor(name, shape, dt))

        def sem(name):
            return ctx.enter_context(nc.semaphore(name))

        cst = sb("cst", [P, 256], F32)
        gu = sb("gu", [P, 3, 8, 512], F16)
        dw = sb("dw", [P, NI, 512], F32R)
        wf = sb("wf", [P, 2, 2, KT, 512], F32R)
        wo = sb("wo", [P, 2, KT, 512], F32R)
        xTr = sb("xTr", [P, 2, 512], F32)
        xTs = sb("xTs", [P, 2, KT, 512], F32R)
        qk = sb("qk", [P, NT, 2, 512], F32)
        ks = sb("ks", [P, 2, NT, 512], F16)
        tu = sb("tu", [P, 2, 512], F32)
        pT = sb("pT", [P, 2, 512], F32R)
        h = sb("h", [P, 2, NT, 512], F32)
        hT = sb("hT", [P, 2, 2, KT, 512], F16)
        fu = sb("fu", [P, 2, 2, 512], F32R)
        sl = sb("sl", [P, 2, 512], F32)
        ff = sb("ff", [P, 2, 512], F32)
        ds = sb("ds", [P, 512], F32)
        gs = sb("gs", [P, NI], F32)
        us = sb("us", [P, NI], F32)
        tr16 = sb("tr16", [P, 2, P], F16)
        mq = sb("mq", [P, 2, 512], BF16)
        bst = sb("bst", [P, 8, 6], F32)
        mv1 = sb("mv1", [P, NT, 2], F32)
        mv2 = sb("mv2", [P, NT, 2], F32)
        S = sb("S", [P, NT, 32], F32)
        E, Q, y0, ya, yy = (sb(n, [P, NT, 33], F32) for n in ("E", "Q", "y0", "ya", "yy"))
        rv = sb("rv", [P, NT], F32)
        sc = sb("sc", [P, NT, 32], F32)
        E2 = sb("E2", [P, 5, NT], F32)
        wst = sb("wst", [P, 8, 6], F32)
        wmv = sb("wmv", [P, 8, 2], F32)

        fwd = cst[:, 0:128].rearrange("p (a c) -> p a c", a=2)
        ident = cst[:, 128:256]
        cst2 = sl[:, :, :].rearrange("p a n -> p (a n)")[:, 0:768]
        inv = cst2[:, 0:512].rearrange("p (a c) -> p a c", a=4)
        stage = hT[:, 1, :, :, :].rearrange("p a k n -> p (a k n)").bitcast(F32).rearrange("p (s n) -> p s n", s=4)
        raw = [hT[:, 0, :, :, :].rearrange("p a k n -> p (a k n)").bitcast(F32).rearrange("p (s n) -> p s n", s=4),
               gu[:, 1, :, :].rearrange("p k n -> p (k n)").bitcast(F32).rearrange("p (s n) -> p s n", s=4)]
        woR = gu[:, 2, :, :].rearrange("p k n -> p (k n)").bitcast(F32).rearrange("p (s n) -> p s n", s=4)

        def bank(name):
            return ctx.enter_context(nc.psum_tensor(name, [P, 512], F32))

        bd = [bank(f"bd{i}") for i in range(NT)]
        bg, bu = bank("bg"), bank("bu")
        ba = [bank("ba0"), bank("ba1")] + [bg, bu] + bd

        pe, act, dve, pool = (Line(sem(n)) for n in ("s_pe", "s_act", "s_dve", "s_pool"))
        sp = Line(sem("s_sp"))

        sent = {}

        def dma(dst, src, name, *after):
            if name not in sent:
                sent[name] = [sem("d_" + name), 0]
            s = sent[name]
            s[1] += 16
            sp.do(lambda e: e.dma_start(dst, src).then_inc(s[0], 16), *after, mark=False)
            return (s[0], s[1])

        a_free = [[] for _ in ba]
        a_next, a_banks = [0], [8]

        def a_bank():
            i = a_next[0] % a_banks[0]
            a_next[0] += 1
            return i

        xtr_free = [[], []]
        xts_read = []
        t_xts = {}

        t_xtr = {}

        def load_xT(b, k):
            slot = k % 2
            src = xT[P * k:P * k + P, D * b:D * b + D]
            if b == 0:
                t_xtr[b, k] = dma(h[:, 1, k, :], src, f"x1{k}")
            else:
                t_xtr[b, k] = dma(xTr[:, slot, :], src, f"xtr{slot}", *xtr_free[slot])

        def split_xT(b, k):
            src = h[:, 1, k, :] if b == 0 else xTr[:, k % 2, :]
            hi = act.do(lambda e: e.activation(xTs[:, 0, k, :], src, ACT.Copy), t_xtr[b, k], *xts_read)
            lo = pool.do(lambda e: e.tensor_tensor(xTs[:, 1, k, :], src, xTs[:, 0, k, :].bitcast(F32), ALU.subtract), hi)
            if b == 0:
                h_free[1].append([hi, lo])
            else:
                xtr_free[k % 2] = [hi, lo]
            t_xts[b, k] = lo

        t_x = {}
        h_free = [[], []]
        t_mv1 = {}
        mv1_read = []

        def load_x(b):
            for t in range(NT):
                after = h_free[b % 2][t] if h_free[b % 2] else ()
                t_x[b, t] = dma(h[:, b % 2, t, :], x[D * b + P * t:D * b + P * t + P, :], f"x{b % 2}{t}", *after)

        def stats1(b, t):
            st = dve.do(lambda e: e.bn_stats(bst[:, t, :], h[:, b % 2, t, :]), t_x[b, t])
            t_mv1[b, t] = dve.do(lambda e: e.bn_aggr(mv1[:, t, :], bst[:, t, :]), st)

        qk_free = {}
        t_S = {}
        t_qk = {}
        sq_free = []

        def qk_piece(b, t):
            nonlocal sq_free
            done = []
            sqs = []
            for w in range(2):
                i = a_bank()
                first = True
                for k in range(KT):
                    for part_x, part_w in ((0, 0), (0, 1), (1, 0)):
                        last = k == KT - 1 and part_x == 1
                        pe_t = pe.do(lambda e, w=w, k=k, part_x=part_x, part_w=part_w, first=first, last=last, i=i: e.matmul(
                            ba[i][:, :], xTs[:, part_x, k, P * t:P * t + P], wf[:, w, part_w, k, :],
                            start=first, stop=last),
                            *(([*a_free[i]] + [t_xts[b, kk] for kk in range(KT)] + t_wf[w]) if first else []), mark=last)
                        first = False
                sq = act.do(lambda e, i=i, w=w: e.activation(tu[:, w, :], ba[i][:, :], ACT.Square), pe_t, *sq_free)
                cp = act.do(lambda e, i=i, w=w: e.activation(qk[:, t, w, :], ba[i][:, :], ACT.Copy),
                            *qk_free.get((t, w), []))
                a_free[i] = [cp]
                sqs.append(sq)
                done.append(cp)
            if t == NT - 1:
                xts_read[:] = [pe_t]
            for w in range(2):
                v = tu[:, w, :].rearrange("p (a c j) -> p c a j", a=2, c=NH)
                red = dve.do(lambda e, w=w, v=v: e.tensor_reduce(S[:, t, NH * w:NH * w + NH], v, AX.XY, ALU.add), sqs[w])
            sq_free = [red]
            t_S[b, t] = red
            t_qk[b, t] = done

        def refined_rsqrt(e_ap, q_ap, y_ap, a_ap, out_ap, ready, q_read):
            sq = act.do(lambda e: e.activation(q_ap, e_ap, ACT.Sqrt), ready, *q_read)
            r = dve.do(lambda e: e.reciprocal(y_ap, q_ap), sq)
            a = dve.do(lambda e: e.scalar_tensor_tensor(out=a_ap, in0=y_ap, scalar=-0.5, in1=y_ap,
                                                        op0=ALU.mult, op1=ALU.mult), r)
            b = dve.do(lambda e: e.tensor_tensor(a_ap, a_ap, e_ap, ALU.mult), a)
            return dve.do(lambda e: e.scalar_tensor_tensor(out=out_ap, in0=a_ap, scalar=1.5, in1=y_ap,
                                                           op0=ALU.add, op1=ALU.mult), b)

        t_sc = {}

        def norm_piece(b, ts):
            g = slice(ts[0], ts[-1] + 1)
            n = len(ts)
            ve = dve.do(lambda e: e.tensor_scalar(E[:, g, 0], mv1[:, g, 1], EPS, None, ALU.add), t_mv1[b, ts[-1]])
            r = dve.do(lambda e: e.reciprocal(rv[:, g], E[:, g, 0]), ve)
            ss = dve.do(lambda e: e.tensor_tensor(E[:, g, 1:33], S[:, g, :], rv[:, g].unsqueeze(2).broadcast_to([P, n, 32]),
                                                  ALU.mult), r, t_S[b, ts[-1]])
            y = refined_rsqrt(E[:, g, :], Q[:, g, :], y0[:, g, :], ya[:, g, :], yy[:, g, :], ss, [])
            m = dve.do(lambda e: e.tensor_tensor(sc[:, g, :], yy[:, g, 1:33], yy[:, g, 0:1].broadcast_to([P, n, 32]),
                                                 ALU.mult), y)
            for t in ts:
                t_sc[b, t] = m

        t_qn = {}
        t_ks = {}
        ks_free = {}

        def head_scale(t, w):
            return sc[:, t, NH * w:NH * w + NH].unsqueeze(1).unsqueeze(3).broadcast_to([P, 2, NH, 16])

        def split_heads(ap):
            return ap.rearrange("p (a c j) -> p a c j", a=2, c=NH)

        def scale_piece(b, t):
            kn = dve.do(lambda e: e.tensor_tensor(split_heads(qk[:, t, 1, :]), split_heads(qk[:, t, 1, :]),
                                                  head_scale(t, 1), ALU.mult), t_sc[b, t], t_qk[b, t][1])
            hi = act.do(lambda e: e.activation(ks[:, 0, t, :], qk[:, t, 1, :], ACT.Copy), kn, *ks_free.get(t, []))
            lo = pool.do(lambda e: e.tensor_tensor(ks[:, 1, t, :], qk[:, t, 1, :], ks[:, 0, t, :], ALU.subtract), hi)
            t_qn[b, t] = dve.do(lambda e: e.tensor_tensor(split_heads(qk[:, t, 0, :]), split_heads(qk[:, t, 0, :]),
                                                          head_scale(t, 0), ALU.mult), t_qk[b, t][0])
            t_ks[b, t] = lo

        t_p = {}
        tu_free = [[]]

        def tri_piece(b, t):
            nonlocal sq_free
            i = a_bank()
            for s in range(t + 1):
                for part in range(2):
                    first, last = s == 0 and part == 0, s == t and part == 1
                    c = pe.do(lambda e, s=s, part=part, first=first, last=last: e.matmul(
                        ba[i][:, :], tr16[:, 0 if s == t else 1, :], ks[:, part, s, :], start=first, stop=last),
                        *(([*a_free[i]] + [t_ks[b, t], t_tr16]) if first else []), mark=last)
            if t == NT - 1:
                for s in range(NT):
                    ks_free[s] = [c]
            qn = qk[:, t, 0, :]
            T, U = tu[:, 0, :], tu[:, 1, :]
            tt = dve.do(lambda e: e.tensor_tensor(T, qn, ba[i][:, :], ALU.mult), c, t_qn[b, t], *tu_free[0], *sq_free)
            dve.do(lambda e: e.tensor_tensor(U[:, 0:256], qn[:, 0:256], ba[i][:, 256:512], ALU.mult))
            u = dve.do(lambda e: e.tensor_tensor(U[:, 256:512], qn[:, 256:512], ba[i][:, 0:256], ALU.mult))
            a_free[i] = [u]
            r = pool.do(lambda e: e.tensor_tensor(qn[:, 0:256], T[:, 0:256], T[:, 256:512], ALU.subtract), u)
            m = pool.do(lambda e: e.tensor_tensor(qn[:, 256:512], U[:, 0:256], U[:, 256:512], ALU.add))
            z = pool.do(lambda e: e.tensor_copy(split_heads(qn)[:, :, :, 0], split_heads(T)[:, :, :, 0]), r, m)
            tu_free[0] = [z]
            sq_free = [z]
            t_p[b, t] = z

        pTs = [pT[:, :, :], fu[:, 0, :, :], fu[:, 1, :, :]]
        pT_free = [[], [], []]
        pT_next, pT_bufs = [0], [3]
        pT_at = {}
        t_pT = {}

        def pt_piece(b, t):
            i = a_bank()
            for j in range(KT):
                tp = pe.do(lambda e, j=j: e.transpose(ba[i][:, P * j:P * j + P], qk[:, t, 0, P * j:P * j + P], ident),
                           *([*a_free[i], t_p[b, t]] if j == 0 else []), mark=j == KT - 1)
            qk_free[t, 0] = [tp]
            n = pT_next[0] % pT_bufs[0]
            pT_next[0] += 1
            pT_at[b, t] = n
            dst = pTs[n]
            hi = act.do(lambda e: e.activation(dst[:, 0, :], ba[i][:, :], ACT.Copy), tp, *pT_free[n])
            lo = dve.do(lambda e: e.tensor_tensor(dst[:, 1, :], ba[i][:, :], dst[:, 0, :].bitcast(F32), ALU.subtract), hi)
            a_free[i] = [lo]
            t_pT[b, t] = lo

        t_h = {}
        t_mv2 = {}

        def o_piece(b, t):
            i = a_bank()
            first = True
            src = pTs[pT_at[b, t]]
            for j in range(KT):
                for part_p, part_w in ((0, 0), (0, 1), (1, 0)):
                    last = j == KT - 1 and part_p == 1
                    o = pe.do(lambda e, j=j, part_p=part_p, part_w=part_w, first=first, last=last: e.matmul(
                        ba[i][:, :], src[:, part_p, P * j:P * j + P], wo[:, part_w, j, :], start=first, stop=last),
                        *(([*a_free[i], t_pT[b, t]] + t_wo) if first else []), mark=last)
                    first = False
            pT_free[pT_at[b, t]] = [o]
            hh = h[:, b % 2, t, :]
            t_h[b, t] = dve.do(lambda e: e.tensor_tensor(hh, ba[i][:, :], hh, ALU.add), o, t_x[b, t])
            a_free[i] = [t_h[b, t]]
            st = dve.do(lambda e: e.bn_stats(bst[:, 4 + t, :], hh), t_h[b, t])
            t_mv2[b, t] = dve.do(lambda e: e.bn_aggr(mv2[:, t, :], bst[:, 4 + t, :]), st)

        t_r2 = {}

        def ln2_piece(b, ts):
            g = slice(ts[0], ts[-1] + 1)
            ve = dve.do(lambda e: e.tensor_scalar(E2[:, 0, g], mv2[:, g, 1], EPS, None, ALU.add), t_mv2[b, ts[-1]])
            r = refined_rsqrt(E2[:, 0, g], E2[:, 1, g], E2[:, 2, g], E2[:, 3, g], E2[:, 4, g], ve, [])
            for t in ts:
                t_r2[b, t] = r

        t_hT = {}
        hT_free = [[], []]

        t_hn = {}

        def hn_piece(b, t):
            hn = qk[:, t, 1, :]
            t_hn[b, t] = dve.do(lambda e: e.tensor_scalar(hn, h[:, b % 2, t, :], mv2[:, t, 0:1], E2[:, 4, t:t + 1],
                                                          ALU.subtract, ALU.mult), t_r2[b, t], t_ks[b, t])

        def ht_piece(b, t):
            i = a_bank()
            for k in range(KT):
                tp = pe.do(lambda e, k=k: e.transpose(ba[i][:, P * k:P * k + P], qk[:, t, 1, P * k:P * k + P], ident),
                           *([*a_free[i], t_hn[b, t]] if k == 0 else []), mark=k == KT - 1)
            qk_free[t, 1] = [tp]
            src = ba[i][:, :].rearrange("p (k n) -> p k n", k=KT)
            hi_ap = hT[:, b % 2, 0, :, P * t:P * t + P]
            lo_ap = hT[:, b % 2, 1, :, P * t:P * t + P]
            hi = act.do(lambda e: e.activation(hi_ap, src, ACT.Copy), tp, *hT_free[b % 2])
            lo = dve.do(lambda e: e.tensor_tensor(lo_ap, src, hi_ap, ALU.subtract), hi)
            a_free[i] = [lo]
            t_hT[b, t] = lo

        t_silu = {}
        t_f = {}
        ff_free = [[], []]
        ff_next = [0]
        pending = []
        g_free, u_free = [], []
        fu_free = [[], []]
        t_fu = {}

        def gu_piece(b, i):
            nonlocal g_free, u_free
            c, col = i // 4, P * (i % 4)
            n = b * NI + i
            for w, bk, free in ((0, bg, g_free), (1, bu, u_free)):
                for k in range(KT):
                    for part in range(2):
                        first, last = k == 0 and part == 0, k == KT - 1 and part == 1
                        m = pe.do(lambda e, w=w, bk=bk, k=k, part=part, first=first, last=last: e.matmul(
                            bk[:, :], gu[:, c, 4 * w + k, col:col + P], hT[:, b % 2, part, k, :], start=first, stop=last),
                            *((free + [t_hT[b, t] for t in range(NT)] + t_gu[c]) if first else []), mark=last)
                if w == 0:
                    tg = m
                else:
                    tu_ = m
            if i == NI - 1:
                hT_free[b % 2] = [tu_]
            s = sl[:, n % 2, :]
            r = ff_next[0] % 2
            ff_next[0] += 1
            f = ff[:, r, :]
            si = act.do(lambda e: e.activation(s, bg[:, :], ACT.Silu, scale=gs[:, i:i + 1]), tg, t_sc_load,
                        *([t_f[n - 2]] if n >= 2 else wo_raw_read))
            g_free = [si]
            t_f[n] = dve.do(lambda e: e.scalar_tensor_tensor(out=f, in0=bu[:, :], scalar=us[:, i:i + 1], in1=s,
                                                             op0=ALU.mult, op1=ALU.mult), tu_, si, *ff_free[r])
            u_free = [t_f[n]]
            pending.append((n, r, f))

        def split_f():
            n, r, f = pending.pop()
            hi = act.do(lambda e: e.activation(fu[:, n % 2, 0, :], f, ACT.Copy), t_f[n], *fu_free[n % 2])
            lo = dve.do(lambda e: e.tensor_tensor(fu[:, n % 2, 1, :], f, fu[:, n % 2, 0, :].bitcast(F32), ALU.subtract), hi)
            ff_free[r] = [hi, lo]
            t_fu[n] = lo

        d_free = [[] for _ in range(NT)]
        t_d = {}

        def d_piece(b, i):
            n = b * NI + i
            for t in range(NT):
                for part in range(2):
                    t_d[t] = pe.do(lambda e, t=t, part=part: e.matmul(
                        bd[t][:, :], fu[:, n % 2, part, P * t:P * t + P], dw[:, i, :],
                        start=i == 0 and part == 0, stop=i == NI - 1 and part == 1),
                        *((([t_fu[n]] + t_dw[i]) if t == 0 else []) + (d_free[t] if i == 0 else []) if part == 0 else []),
                        mark=part == 1)
            fu_free[n % 2] = [t_d[NT - 1]]

        def fin_piece(b):
            freed = []
            for t in range(NT):
                r = ff_next[0] % 2
                ff_next[0] += 1
                y = ff[:, r, :]
                hh = h[:, b % 2, t, :]
                m = dve.do(lambda e, t=t, y=y: e.tensor_tensor(y, bd[t][:, :], ds[:, :], ALU.mult), t_d[t], t_sc_load, *ff_free[r])
                d_free[t] = [m]
                on = dve if b == NB - 1 else pool
                a = on.do(lambda e, y=y, hh=hh: e.tensor_tensor(hh, y, hh, ALU.add), m)
                ff_free[r] = [a]
                freed.append([dma(out[D * b + P * t:D * b + P * t + P, :], hh, f"o{b % 2}{t}", a)])
            h_free[b % 2] = freed

        chunks = []
        for c in range(3):
            for w, src in ((0, gate_w), (1, up_w)):
                for k in range(KT):
                    chunks.append((src[P * k:P * k + P, 512 * c:512 * c + 512], gu[:, c, 4 * w + k, :], c, None))
            for i in range(4 * c, 4 * c + 4):
                chunks.append((down_w[P * i:P * i + P, :], dw[:, i, :], c, i))
        t_gu = {c: [] for c in range(3)}
        t_dw = {}
        st_free = [[] for _ in range(4)]
        t_st = {}
        mq_free = [[], []]

        def load_chunk(n):
            t_st[n] = dma(stage[:, n % 4, :], chunks[n][0], f"st{n % 4}", *st_free[n % 4])

        quant_next = [0]

        def quant(*on):
            ns = range(quant_next[0], quant_next[0] + len(on))
            quant_next[0] += len(on)
            e1, e2 = {}, {}
            for n in ns:
                top = stage[:, n % 4, :].bitcast(U16).rearrange("p (n t) -> p n t", t=2)[:, :, 1]
                e1[n] = dve.do(lambda e, n=n, top=top: e.tensor_scalar(mq[:, n % 2, :].bitcast(U16), top, 0x7F80, 0x0040,
                                                                       ALU.bitwise_and, ALU.bitwise_or),
                               t_st[n], *mq_free[n % 2])
            for n in ns:
                e2[n] = dve.do(lambda e, n=n: e.tensor_scalar(mq[:, n % 2, :], mq[:, n % 2, :], 1.5 * 2.0 ** -6, 2.0 ** 20,
                                                              ALU.max, ALU.mult), e1[n])
            for n, eng in zip(ns, on):
                _, dst, c, i = chunks[n]
                w, m = stage[:, n % 4, :], mq[:, n % 2, :]
                after = wo_raw_read if (i is None and c == 2) else raw_read[1] if (i is None and c == 1) else []
                a = eng.do(lambda e, w=w, m=m: e.tensor_tensor(w, w, m, ALU.add), e2[n])
                b = eng.do(lambda e, w=w, m=m, dst=dst: e.tensor_tensor(dst, w, m, ALU.subtract), a, *after)
                mq_free[n % 2] = [b]
                st_free[n % 4] = [b]
                if i is None:
                    t_gu[c].append(b)
                else:
                    t_dw[i] = [b]
                if n + 4 < len(chunks):
                    load_chunk(n + 4)
                else:
                    hT_free[1].append(b)

        t_cst = dma(cst[:, :], cst_d, "cst")
        t_cst2 = dma(cst2, cst2_d, "cst2")
        t_raw = {}
        for w, src in ((0, w_q), (1, w_kv)):
            for f in range(KT):
                t_raw[w, f] = dma(raw[w][:, f, :], src[P * f:P * f + P, :], f"raw{w}{f}")
            if w == 0:
                for k in range(KT):
                    load_xT(0, k)
        load_chunk(0)
        load_chunk(1)
        load_x(0)
        load_chunk(2)
        load_chunk(3)
        t_woR = dma(woR, woT.rearrange("(f p) n -> p f n", p=P), "woR")
        load_xT(1, 0)
        load_xT(1, 1)
        dma(gs[:, :], gs_d, "sc")
        dma(us[:, :], us_d, "sc")
        t_sc_load = dma(ds[:, :], ds_d.rearrange("(a n) -> a n", a=1).broadcast_to([P, D]), "sc")

        t_tr16 = act.do(lambda e: e.activation(tr16[:, :, :], cst2[:, 512:768].rearrange("p (a n) -> p a n", a=2), ACT.Copy),
                        t_cst2)

        t_wf = [[], []]
        raw_read = [[], []]
        wo_raw_read = []

        def center(w):
            js = [(f, KT * w + f) for f in range(KT)]
            st = [dve.do(lambda e, f=f, j=j: e.bn_stats(wst[:, j, :], raw[w][:, f, :]), t_raw[w, f]) for f, j in js]
            ag = [dve.do(lambda e, j=j: e.bn_aggr(wmv[:, j, :], wst[:, j, :]), st[f]) for f, j in js]
            return [dve.do(lambda e, f=f, j=j: e.tensor_scalar(raw[w][:, f, :], raw[w][:, f, :], wmv[:, j, 0:1], None,
                                                               ALU.subtract), ag[f]) for f, j in js]

        def transform(w, t_c):
            for k in range(KT):
                i = a_bank()
                view = ba[i][:, :].rearrange("p (a n) -> p a n", a=2)
                for f in range(KT):
                    m = pe.do(lambda e, f=f, view=view, k=k: e.matmul(view[:, :, 64 * f:64 * f + 64], raw[w][:, f, P * k:P * k + P],
                                                                     fwd, start=True, stop=True),
                              *(a_free[i] + [t_cst] if f == 0 else []), *([t_c[f]] if k == 0 else []), mark=f == KT - 1)
                hi = act.do(lambda e, i=i, k=k: e.activation(wf[:, w, 0, k, :], ba[i][:, :], ACT.Copy), m)
                lo = dve.do(lambda e, i=i, k=k: e.tensor_tensor(wf[:, w, 1, k, :], ba[i][:, :],
                                                                wf[:, w, 0, k, :].bitcast(F32), ALU.subtract), hi)
                a_free[i] = [lo]
                t_wf[w] = [lo]
                raw_read[w] = [m]

        t_wo = []

        def transform_o():
            for j in range(KT):
                part, half = j // 2, j % 2
                i = a_bank()
                for par in range(2):
                    m = pe.do(lambda e, i=i, par=par, part=part, half=half: e.matmul(
                        ba[i][:, :], inv[:, 2 * par + part, :], woR[:, 2 * half + par, :], start=par == 0, stop=par == 1),
                        *(a_free[i] + [t_woR, t_cst2] if par == 0 else []), mark=par == 1)
                hi = act.do(lambda e, i=i, j=j: e.activation(wo[:, 0, j, :], ba[i][:, :], ACT.Copy), m)
                lo = dve.do(lambda e, i=i, j=j: e.tensor_tensor(wo[:, 1, j, :], ba[i][:, :],
                                                                wo[:, 0, j, :].bitcast(F32), ALU.subtract), hi)
                a_free[i] = [lo]
                t_wo[:] = [lo]
                wo_raw_read[:] = [m]

        for k in range(KT):
            split_xT(0, k)
        t_c = [center(0), center(1)]
        transform(0, t_c[0])
        quant(pool, pool)
        transform(1, t_c[1])
        hT_free[0] = raw_read[0]
        quant(pool, pool)
        for t in range(NT):
            stats1(0, t)
        quant(pool, pool)
        qk_piece(0, 0)
        qk_piece(0, 1)
        norm_piece(0, [0, 1])
        scale_piece(0, 0)
        scale_piece(0, 1)
        quant(pool, pool)
        qk_piece(0, 2)
        qk_piece(0, 3)
        norm_piece(0, [2, 3])
        scale_piece(0, 2)
        scale_piece(0, 3)
        tri_piece(0, 0)
        tri_piece(0, 1)
        load_x(1)
        transform_o()
        pt_piece(0, 0)
        tri_piece(0, 2)
        pt_piece(0, 1)
        o_piece(0, 0)
        tri_piece(0, 3)
        quant(pool, pool)
        o_piece(0, 1)
        pt_piece(0, 2)
        split_xT(1, 0)
        split_xT(1, 1)
        load_xT(1, 2)
        load_xT(1, 3)
        ln2_piece(0, [0, 1])
        hn_piece(0, 0)
        hn_piece(0, 1)
        pt_piece(0, 3)
        o_piece(0, 2)
        ht_piece(0, 0)
        o_piece(0, 3)
        ht_piece(0, 1)
        quant(pool, pool)
        ln2_piece(0, [2, 3])
        hn_piece(0, 2)
        hn_piece(0, 3)
        ht_piece(0, 2)
        ht_piece(0, 3)
        split_xT(1, 2)
        split_xT(1, 3)

        a_banks[0] = 2
        pT_bufs[0] = 1
        fu_free[:] = pT_free[1:]
        g_free, u_free = a_free[2], a_free[3]
        for t in range(NT):
            d_free[t] = a_free[4 + t]
        def before_d(b, slot):
            if slot in (0, 1):
                qk_piece(b, slot)
            if slot == 2:
                qk_piece(b, 3)
            if 6 <= slot <= 9:
                o_piece(b, slot - 6)
            if 5 <= slot <= 8:
                pt_piece(b, slot - 5)
            if slot == 10:
                ht_piece(b, 0)
                ht_piece(b, 1)
            if slot == 11:
                ht_piece(b, 3)

        def behind_d(b, slot):
            if slot == 1:
                qk_piece(b, 2)
                for t in range(NT):
                    stats1(b, t)
            if slot == 2:
                norm_piece(b, range(NT))
            if slot == 3:
                scale_piece(b, 0)
                scale_piece(b, 1)
            if slot == 4:
                scale_piece(b, 2)
                scale_piece(b, 3)
            if 4 <= slot <= 7:
                tri_piece(b, slot - 4)
            if slot == 9:
                ln2_piece(b, range(NT))
                for t in range(NT):
                    hn_piece(b, t)
            if slot == 10:
                ht_piece(b, 2)

        for b in range(NB):
            for i in range(NI):
                gu_piece(b, i)
                if b + 1 < NB:
                    before_d(b + 1, i)
                if b == 0 and i < 3:
                    quant(pool, dve)
                if (b, i) != (0, 0):
                    d_piece(*divmod(b * NI + i - 1, NI))
                split_f()
                if b + 1 < NB:
                    behind_d(b + 1, i)
                if i == 0 and b > 0:
                    fin_piece(b - 1)
                    if b + 1 < NB:
                        load_x(b + 1)
                if b + 2 < NB:
                    if i == 4:
                        load_xT(b + 2, 0)
                        load_xT(b + 2, 1)
                    if 6 <= i < 10:
                        split_xT(b + 2, i - 6)
                        if i < 8:
                            load_xT(b + 2, i - 4)
                if b == 0 and i < 9:
                    quant(pool, dve)
        d_piece(NB - 1, NI - 1)
        fin_piece(NB - 1)
        for name, s in sent.items():
            if name[0] == "o":
                sp.do(lambda e: e.nop(), (s[0], s[1]), mark=False)

        with nc.Block() as block:
            @block.sync
            def _(e):
                sp.run(e)

            @block.tensor
            def _(e):
                pe.run(e)

            @block.scalar
            def _(e):
                act.run(e)

            @block.vector
            def _(e):
                dve.run(e)

            @block.gpsimd
            def _(e):
                pool.run(e)


def kernel(L0_attn_x, L0_attn_W_q, L0_attn_W_kv, L0_attn_W_o, L0_ffn_gate_w, L0_ffn_up_w, L0_ffn_down_w,
           L0_ffn_gate_scale, L0_ffn_up_scale, L0_ffn_down_scale):
    import concourse.bacc as bacc
    from concourse.bass_utils import run_bass_kernel_spmd

    x = np.ascontiguousarray(np.asarray(L0_attn_x).reshape(NB * D, D))
    cst, cst2 = constants()
    arrays = {
        "x": x,
        "xT": np.ascontiguousarray(x.T),
        "w_q": np.ascontiguousarray(L0_attn_W_q),
        "w_kv": np.ascontiguousarray(L0_attn_W_kv),
        "woT": np.ascontiguousarray(np.asarray(L0_attn_W_o).T),
        "gate_w": np.ascontiguousarray(L0_ffn_gate_w),
        "up_w": np.ascontiguousarray(L0_ffn_up_w),
        "down_w": np.ascontiguousarray(L0_ffn_down_w),
        "gs": np.ascontiguousarray(np.asarray(L0_ffn_gate_scale).reshape(NI, P).T),
        "us": np.ascontiguousarray(np.asarray(L0_ffn_up_scale).reshape(NI, P).T),
        "ds": np.ascontiguousarray(L0_ffn_down_scale),
        "cst": cst,
        "cst2": cst2,
    }
    nc = bacc.Bacc("TRN2", target_bir_lowering=False, num_devices=1)
    args = [nc.dram_tensor(n + "_dram", a.shape, mybir.dt.from_np(a.dtype), kind="ExternalInput").ap()
            for n, a in arrays.items()]
    out = nc.dram_tensor("out_dram", (NB * D, D), F32, kind="ExternalOutput").ap()
    build(nc, *args, out)
    r = run_bass_kernel_spmd(nc, [{n + "_dram": a for n, a in arrays.items()}], core_ids=[0])
    return r.results[0]["out_dram"].reshape(NB, D, D)
```

```python
import numpy as np
import concourse.bass as bass
from concourse import mybir
from contextlib import ExitStack

F32 = mybir.dt.float32
F32R = mybir.dt.float32r
F16 = mybir.dt.float16
BF16 = mybir.dt.bfloat16
U16 = mybir.dt.uint16
ALU = mybir.AluOpType
ACT = mybir.ActivationFunctionType
AX = mybir.AxisListType

P = 128
NB = 4
NT = 4
KT = 4
D = 512
NI = 12
NH = 16
HD = 32
EPS = 1e-5


def constants():
    n = np.arange(HD)[:, None]
    j = np.arange(16)[None, :]
    ang = 2.0 * np.pi * n * j / HD
    alt = np.where(n[:, 0] % 2 == 0, 1.0, -1.0)
    fre, fim = np.sqrt(2.0) * np.cos(ang), -np.sqrt(2.0) * np.sin(ang)
    fre[:, 0], fim[:, 0] = 1.0, alt
    ire, iim = np.cos(ang) / HD, -np.sin(ang) / HD
    ire[:, 0], iim[:, 0] = 1.0 / HD, alt / HD
    fwd = np.zeros((P, P))
    inv = np.zeros((P, P))
    for h in range(4):
        r = slice(HD * h, HD * h + HD)
        fwd[r, r] = np.concatenate([fre, fim], 1)
        inv[r, r] = np.concatenate([ire, iim], 1)
    ident = np.eye(P)
    tri = np.triu(np.ones((P, P)))
    ones = np.ones((P, P))
    return (np.concatenate([fwd, ident], 1).astype(np.float32),
            np.concatenate([inv, tri, ones], 1).astype(np.float32))


ROUNDING = {
    "a1": "eepep", "a2": "eepp", "a3": "ee", "a4": "pp", "a5": "e",
    "p1": "e", "p2": "d", "p8": "p", "p9": "p", "p11": "e", "p12": "epd", "gu0": "epe", "split0": "ep", "end0": "ed",
    "gu1": "pe", "q10": "eep", "q11": "peed", "split1": "e", "stats": "ppp", "end1": "epe", "gu2": "p", "q30": "ep",
    "kv0": "ee", "end3": "p", "gu4": "p", "split4": "eed", "end4": "e", "kv1": "p", "end5": "e", "gu6": "ed",
    "kv2": "p", "end6": "de", "gu7": "de", "kv3": "e", "split7": "p", "end7": "ep", "split8": "ep", "gu9": "p",
}


class Line:

    def __init__(self, sem):
        self.sem, self.n, self.q = sem, 0, []

    def do(self, fn, *after, mark=True):
        self.q.append((fn, after, mark))
        if mark:
            self.n += 1
        return (self.sem, self.n)

    def run(self, eng):
        for fn, after, mark in self.q:
            for sem, value in after:
                eng.wait_ge(sem, value)
            ins = fn(eng)
            if mark:
                ins.then_inc(self.sem, 1)


def build(nc, x, xT, w_q, w_kv, woT, gate_w, up_w, down_w, gs_d, us_d, ds_d, cst_d, cst2_d, out):
    ctx = ExitStack()
    with ctx:
        def sb(name, shape, dt):
            return ctx.enter_context(nc.sbuf_tensor(name, shape, dt))

        def sem(name):
            return ctx.enter_context(nc.semaphore(name))

        cst = sb("cst", [P, 256], F32)
        gu = sb("gu", [P, 3, 8, 512], F16)
        dw = sb("dw", [P, NI, 512], F32R)
        wf = sb("wf", [P, 2, 2, KT, 512], F32R)
        wo = sb("wo", [P, 2, KT, 512], F32R)
        xTr = sb("xTr", [P, 2, 512], F32)
        xTs = sb("xTs", [P, 2, KT, 512], F32R)
        qk = sb("qk", [P, NT, 2, 512], F32)
        ks = sb("ks", [P, 2, NT, 512], F16)
        tu = sb("tu", [P, 2, 512], F32)
        pT = sb("pT", [P, 2, 512], F32R)
        h = sb("h", [P, 2, NT, 512], F32)
        hT = sb("hT", [P, 2, 2, KT, 512], F16)
        fu = sb("fu", [P, 2, 2, 512], F32R)
        sl = sb("sl", [P, 2, 512], F32)
        ff = sb("ff", [P, 2, 512], F32)
        ds = sb("ds", [P, 512], F32)
        gs = sb("gs", [P, NI], F32)
        us = sb("us", [P, NI], F32)
        tr16 = sb("tr16", [P, 2, P], F16)
        minus = sb("minus", [P, P], F32R)
        mq = sb("mq", [P, 3, 512], BF16)
        bst = sb("bst", [P, 8, 6], F32)
        mv1 = sb("mv1", [P, NT, 2], F32)
        mv2 = sb("mv2", [P, NT, 2], F32)
        S = sb("S", [P, NT, 32], F32)
        E, Q, y0, ya, yy = (sb(n, [P, NT, 33], F32) for n in ("E", "Q", "y0", "ya", "yy"))
        rv = sb("rv", [P, NT], F32)
        sc = sb("sc", [P, NT, 32], F32)
        E2 = sb("E2", [P, 5, NT], F32)
        wst = sb("wst", [P, 8, 6], F32)
        wmv = sb("wmv", [P, 8, 2], F32)

        fwd = cst[:, 0:128]
        ident = cst[:, 128:256]
        cst2 = sl[:, :, :].rearrange("p a n -> p (a n)")[:, 0:384]
        inv = cst2[:, 0:128]
        stage = hT[:, 1, :, :, :].rearrange("p a k n -> p (a k n)").bitcast(F32).rearrange("p (s n) -> p s n", s=4)
        raw = [hT[:, 0, :, :, :].rearrange("p a k n -> p (a k n)").bitcast(F32).rearrange("p (s n) -> p s n", s=4),
               gu[:, 1, :, :].rearrange("p k n -> p (k n)").bitcast(F32).rearrange("p (s n) -> p s n", s=4)]
        woR = gu[:, 2, :, :].rearrange("p k n -> p (k n)").bitcast(F32).rearrange("p (s n) -> p s n", s=4)

        def bank(name):
            return ctx.enter_context(nc.psum_tensor(name, [P, 512], F32))

        bd = [bank(f"bd{i}") for i in range(NT)]
        bg, bu = bank("bg"), bank("bu")
        ba = [bank("ba0"), bank("ba1")] + [bg, bu] + bd

        pe, act, dve, pool = (Line(sem(n)) for n in ("s_pe", "s_act", "s_dve", "s_pool"))
        sp = Line(sem("s_sp"))

        sent = {}

        def dma(dst, src, name, *after, on=None):
            if name not in sent:
                sent[name] = [sem("d_" + name), 0]
            s = sent[name]
            s[1] += 16
            (on or sp).do(lambda e: e.dma_start(dst, src).then_inc(s[0], 16), *after, mark=False)
            return (s[0], s[1])

        a_free = [[] for _ in ba]
        a_next, a_banks = [0], [8]

        def a_bank():
            i = a_next[0] % a_banks[0]
            a_next[0] += 1
            return i

        xtr_free = [[], []]
        xts_read = []
        t_xts = {}

        t_xtr = {}

        def load_xT(b, k):
            slot = k % 2
            src = xT[P * k:P * k + P, D * b:D * b + D]
            if b == 0:
                t_xtr[b, k] = dma(h[:, 1, k, :], src, f"x1{k}")
            else:
                t_xtr[b, k] = dma(xTr[:, slot, :], src, f"xtr{slot}", *xtr_free[slot])

        def split_xT(b, k, on=pool):
            src = h[:, 1, k, :] if b == 0 else xTr[:, k % 2, :]
            hi = act.do(lambda e: e.activation(xTs[:, 0, k, :], src, ACT.Copy), t_xtr[b, k], *xts_read)
            lo = on.do(lambda e: e.tensor_tensor(xTs[:, 1, k, :], src, xTs[:, 0, k, :].bitcast(F32), ALU.subtract), hi)
            if b == 0:
                h_free[1].append([hi, lo])
            else:
                xtr_free[k % 2] = [hi, lo]
            t_xts[b, k] = lo

        t_x = {}
        h_free = [[], []]
        t_mv1 = {}
        mv1_read = []

        def load_x(b):
            for t in range(NT):
                after = h_free[b % 2][t] if h_free[b % 2] else ()
                t_x[b, t] = dma(h[:, b % 2, t, :], x[D * b + P * t:D * b + P * t + P, :], f"x{b % 2}{t}", *after)

        def stats1(b, t):
            st = dve.do(lambda e: e.bn_stats(bst[:, t, :], h[:, b % 2, t, :]), t_x[b, t])
            t_mv1[b, t] = dve.do(lambda e: e.bn_aggr(mv1[:, t, :], bst[:, t, :]), st)

        qk_free = {}
        t_S = {}
        t_qk = {}
        sq_free = [[], []]

        t_sq = {}

        def spare(b, place):
            if b == 0:
                for what in ROUNDING.get(place, ""):
                    if what == "e":
                        expo()
                    else:
                        rnd(pool if what == "p" else dve)

        def qk_piece(b, t):
            for w in range(2):
                qk_mm(b, t, w)
                qk_sum(b, t, w)
                spare(b - 1, f"q{t}{w}")

        def qk_mm(b, t, w):
            i = a_bank()
            first = True
            for k in range(KT):
                for part_x, part_w in ((0, 0), (0, 1), (1, 0)):
                    after = a_free[i] if first else []
                    if part_x == part_w:
                        after = after + [t_xts[b, k], t_wf[w, k]]
                    last = k == KT - 1 and part_x == 1
                    pe_t = pe.do(lambda e, w=w, k=k, part_x=part_x, part_w=part_w, first=first, last=last, i=i: e.matmul(
                        ba[i][:, :], xTs[:, part_x, k, P * t:P * t + P], wf[:, w, part_w, k, :],
                        start=first, stop=last), *after, mark=last)
                    first = False
            t_sq[b, t, w] = act.do(lambda e, i=i, w=w: e.activation(tu[:, w, :], ba[i][:, :], ACT.Square), pe_t, *sq_free[w])
            cp = act.do(lambda e, i=i, w=w: e.activation(qk[:, t, w, :], ba[i][:, :], ACT.Copy),
                        *qk_free.get((t, w), []))
            a_free[i] = [cp]
            t_qk[b, t, w] = cp
            if t == NT - 1:
                xts_read[:] = [pe_t]

        def qk_sum(b, t, w):
            v = tu[:, w, :].rearrange("p (c j) -> p c j", c=NH)
            red = dve.do(lambda e: e.tensor_reduce(S[:, t, NH * w:NH * w + NH], v, AX.X, ALU.add), t_sq[b, t, w])
            sq_free[w] = [red]
            t_S[b, t] = red

        def refined_rsqrt(e_ap, q_ap, y_ap, a_ap, out_ap, ready, meanwhile=lambda: None):
            sq = act.do(lambda e: e.activation(q_ap, e_ap, ACT.Sqrt), ready)
            meanwhile()
            r = dve.do(lambda e: e.reciprocal(y_ap, q_ap), sq)
            a = dve.do(lambda e: e.scalar_tensor_tensor(out=a_ap, in0=y_ap, scalar=-0.5, in1=y_ap,
                                                        op0=ALU.mult, op1=ALU.mult), r)
            b = dve.do(lambda e: e.tensor_tensor(a_ap, a_ap, e_ap, ALU.mult), a)
            return dve.do(lambda e: e.scalar_tensor_tensor(out=out_ap, in0=a_ap, scalar=1.5, in1=y_ap,
                                                           op0=ALU.add, op1=ALU.mult), b)

        t_sc = {}

        def norm_piece(b, ts, meanwhile=lambda: None):
            g = slice(ts[0], ts[-1] + 1)
            n = len(ts)
            ve = dve.do(lambda e: e.tensor_scalar(E[:, g, 0], mv1[:, g, 1], EPS, None, ALU.add), t_mv1[b, ts[-1]])
            r = dve.do(lambda e: e.reciprocal(rv[:, g], E[:, g, 0]), ve)
            ss = dve.do(lambda e: e.tensor_tensor(E[:, g, 1:33], S[:, g, :], rv[:, g].unsqueeze(2).broadcast_to([P, n, 32]),
                                                  ALU.mult), r, t_S[b, ts[-1]])
            y = refined_rsqrt(E[:, g, :], Q[:, g, :], y0[:, g, :], ya[:, g, :], yy[:, g, :], ss, meanwhile)
            m = dve.do(lambda e: e.tensor_tensor(sc[:, g, :], yy[:, g, 1:33], yy[:, g, 0:1].broadcast_to([P, n, 32]),
                                                 ALU.mult), y)
            for t in ts:
                t_sc[b, t] = m

        t_qn = {}
        t_ks = {}
        ks_free = {}

        def head_scale(t, w):
            return sc[:, t, NH * w:NH * w + NH].unsqueeze(2).broadcast_to([P, NH, HD])

        def split_heads(ap):
            return ap.rearrange("p (c j) -> p c j", c=NH)

        def split_parts(ap):
            v = ap.rearrange("p (c a j) -> p c a j", c=NH, a=2)
            return v[:, :, 0, :], v[:, :, 1, :]

        t_kn = {}
        t_carry = {}

        def scale_kv(b, t):
            kn = dve.do(lambda e: e.tensor_tensor(split_heads(qk[:, t, 1, :]), split_heads(qk[:, t, 1, :]),
                                                  head_scale(t, 1), ALU.mult), t_sc[b, t], t_qk[b, t, 1])
            t_kn[b, t] = kn
            if b == 0 or t == 0:
                split_kv(b, t)

        def split_kv(b, t):
            ready = t_kn[b, t]
            if (b, t) in t_carry:
                ready = pool.do(lambda e: e.tensor_tensor(qk[0:1, t, 1, :], qk[0:1, t, 1, :], qk[0:1, t - 1, 1, :], ALU.add),
                                ready, t_carry[b, t])
            hi = act.do(lambda e: e.activation(ks[:, 0, t, :], qk[:, t, 1, :], ACT.Copy), ready, *ks_free.get(t, []))
            t_ks[b, t] = pool.do(lambda e: e.tensor_tensor(ks[:, 1, t, :], qk[:, t, 1, :], ks[:, 0, t, :], ALU.subtract), hi)

        def scale_q(b, t):
            t_qn[b, t] = dve.do(lambda e: e.tensor_tensor(split_heads(qk[:, t, 0, :]), split_heads(qk[:, t, 0, :]),
                                                         head_scale(t, 0), ALU.mult), t_sc[b, t], t_qk[b, t, 0])

        t_p = {}
        tu_free = [[], []]

        t_c = {}
        t_read = {}

        def tri_piece(b, t):
            tri_mm(b, t)
            product(b, t)

        def tri_mm(b, t):
            i = a_bank()
            tiles = range(t + 1) if b == 0 else (t,)
            for s in tiles:
                for part in range(2):
                    first, last = s == tiles[0] and part == 0, s == t and part == 1
                    c = pe.do(lambda e, s=s, part=part, first=first, last=last: e.matmul(
                        ba[i][:, :], tr16[:, 0 if s == t else 1, :], ks[:, part, s, :], start=first, stop=last),
                        *(([*a_free[i]] + [t_ks[b, t], t_tr16]) if first else []), mark=last)
            if b > 0 or t == NT - 1:
                for s in tiles:
                    ks_free[s] = [c]
            t_c[b, t] = (i, c)
            t_read[b, t] = []
            if b > 0 and t < NT - 1:
                row = act.do(lambda e: e.activation(qk[96:128, t, 1, :], ba[i][96:128, :], ACT.Copy), c)
                t_read[b, t] = [row]
                t_carry[b, t + 1] = dma(qk[0:1, t, 1, :], qk[127:128, t, 1, :], "carry", row, on=act)

        def slot_0(ap):
            return ap.rearrange("p (c j) -> p c j", j=16)[:, :, 0]

        def product(b, t):
            i, c = t_c[b, t]
            qn = qk[:, t, 0, :]
            own = b > 0 or t == 2
            buf = tu if own else ff
            T, U = buf[:, 0, :], buf[:, 1, :]
            tt = dve.do(lambda e: e.tensor_tensor(T, qn, ba[i][:, :], ALU.mult), c, t_qn[b, t], *t_read[b, t],
                        *tu_free[own], *(sq_free[0] + sq_free[1] if own else []))
            (q_re, q_im), (c_re, c_im) = split_parts(qn), split_parts(ba[i][:, :])
            (t_re, t_im), (u_re, u_im) = split_parts(T), split_parts(U)
            dve.do(lambda e: e.tensor_tensor(u_re, q_re, c_im, ALU.mult))
            u = dve.do(lambda e: e.tensor_tensor(u_im, q_im, c_re, ALU.mult))
            a_free[i] = [u]
            r = pool.do(lambda e: e.tensor_tensor(q_re, t_re, t_im, ALU.subtract), u)
            m = pool.do(lambda e: e.tensor_tensor(q_im, u_re, u_im, ALU.add))
            z = pool.do(lambda e: e.tensor_copy(slot_0(qn), slot_0(T)), r, m)
            tu_free[own] = [z]
            if own:
                sq_free[:] = [[z], [z]]
            t_p[b, t] = z

        pTs = [pT[:, :, :], fu[:, 0, :, :], fu[:, 1, :, :]]
        pT_free = [[], [], []]
        pT_next, pT_bufs = [0], [3]
        pT_at = {}
        t_pT = {}

        def pt_piece(b, t):
            i = a_bank()
            for j in range(KT):
                tp = pe.do(lambda e, j=j: e.transpose(ba[i][:, P * j:P * j + P], qk[:, t, 0, P * j:P * j + P], ident),
                           *([*a_free[i], t_p[b, t]] if j == 0 else []), mark=j == KT - 1)
            qk_free[t, 0] = [tp]
            n = pT_next[0] % pT_bufs[0]
            pT_next[0] += 1
            pT_at[b, t] = n
            dst = pTs[n]
            hi = act.do(lambda e: e.activation(dst[:, 0, :], ba[i][:, :], ACT.Copy), tp, *pT_free[n])
            lo = dve.do(lambda e: e.tensor_tensor(dst[:, 1, :], ba[i][:, :], dst[:, 0, :].bitcast(F32), ALU.subtract), hi)
            a_free[i] = [lo]
            t_pT[b, t] = lo

        t_h = {}
        t_mv2 = {}

        def o_piece(b, t):
            i = a_bank()
            first = True
            src = pTs[pT_at[b, t]]
            for j in range(KT):
                for part_p, part_w in ((0, 0), (0, 1), (1, 0)):
                    last = j == KT - 1 and part_p == 1
                    o = pe.do(lambda e, j=j, part_p=part_p, part_w=part_w, first=first, last=last: e.matmul(
                        ba[i][:, :], src[:, part_p, P * j:P * j + P], wo[:, part_w, j, :], start=first, stop=last),
                        *(([*a_free[i], t_pT[b, t]] + t_wo) if first else []), mark=last)
                    first = False
            pT_free[pT_at[b, t]] = [o]
            hh = h[:, b % 2, t, :]
            t_h[b, t] = dve.do(lambda e: e.tensor_tensor(hh, ba[i][:, :], hh, ALU.add), o, t_x[b, t])
            a_free[i] = [t_h[b, t]]
            st = dve.do(lambda e: e.bn_stats(bst[:, 4 + t, :], hh), t_h[b, t])
            t_mv2[b, t] = dve.do(lambda e: e.bn_aggr(mv2[:, t, :], bst[:, 4 + t, :]), st)

        t_r2 = {}

        def ln2_piece(b, ts, meanwhile=lambda: None):
            g = slice(ts[0], ts[-1] + 1)
            ve = dve.do(lambda e: e.tensor_scalar(E2[:, 0, g], mv2[:, g, 1], EPS, None, ALU.add), t_mv2[b, ts[-1]])
            r = refined_rsqrt(E2[:, 0, g], E2[:, 1, g], E2[:, 2, g], E2[:, 3, g], E2[:, 4, g], ve, meanwhile)
            for t in ts:
                t_r2[b, t] = r

        t_hT = {}
        hT_free = [[], []]

        t_hn = {}

        def hn_piece(b, t):
            hn = qk[:, t, 1, :]
            t_hn[b, t] = dve.do(lambda e: e.tensor_scalar(hn, h[:, b % 2, t, :], mv2[:, t, 0:1], E2[:, 4, t:t + 1],
                                                          ALU.subtract, ALU.mult), t_r2[b, t], t_ks[b, NT - 1])

        def ht_piece(b, t):
            i = a_bank()
            for k in range(KT):
                tp = pe.do(lambda e, k=k: e.transpose(ba[i][:, P * k:P * k + P], qk[:, t, 1, P * k:P * k + P], ident),
                           *([*a_free[i], t_hn[b, t]] if k == 0 else []), mark=k == KT - 1)
            qk_free[t, 1] = [tp]
            src = ba[i][:, :].rearrange("p (k n) -> p k n", k=KT)
            hi_ap = hT[:, b % 2, 0, :, P * t:P * t + P]
            lo_ap = hT[:, b % 2, 1, :, P * t:P * t + P]
            hi = act.do(lambda e: e.activation(hi_ap, src, ACT.Copy), tp, *hT_free[b % 2])
            lo = dve.do(lambda e: e.tensor_tensor(lo_ap, src, hi_ap, ALU.subtract), hi)
            a_free[i] = [lo]
            t_hT[b, t] = lo

        t_silu = {}
        t_f = {}
        ff_free = [[], []]
        ff_next = [0]
        pending = []
        g_free, u_free = [], []
        fu_free = [[], []]
        t_fu = {}

        def gu_piece(b, i):
            nonlocal g_free, u_free
            c, col = i // 4, P * (i % 4)
            n = b * NI + i
            for w, bk, free in ((0, bg, g_free), (1, bu, u_free)):
                for k in range(KT):
                    for part in range(2):
                        first, last = k == 0 and part == 0, k == KT - 1 and part == 1
                        m = pe.do(lambda e, w=w, bk=bk, k=k, part=part, first=first, last=last: e.matmul(
                            bk[:, :], gu[:, c, 4 * w + k, col:col + P], hT[:, b % 2, part, k, :], start=first, stop=last),
                            *((free + [t_hT[b, t] for t in range(NT)] + t_gu[c]) if first else []), mark=last)
                if w == 0:
                    tg = m
                else:
                    tu_ = m
            if i == NI - 1:
                hT_free[b % 2] = [tu_]
            s = sl[:, n % 2, :]
            r = ff_next[0] % 2
            ff_next[0] += 1
            f = ff[:, r, :]
            si = act.do(lambda e: e.activation(s, bg[:, :], ACT.Silu, scale=gs[:, i:i + 1]), tg, t_sc_load,
                        *([t_f[n - 2]] if n >= 2 else wo_raw_read))
            g_free = [si]
            t_f[n] = dve.do(lambda e: e.scalar_tensor_tensor(out=f, in0=bu[:, :], scalar=us[:, i:i + 1], in1=s,
                                                             op0=ALU.mult, op1=ALU.mult), tu_, si, *ff_free[r])
            u_free = [t_f[n]]
            pending.append((n, r, f))

        def fu_at(n):
            return (pT[:, :, :], pT_free[0]) if n == NB * NI - 1 else (fu[:, n % 2, :, :], fu_free[n % 2])

        def split_f():
            n, r, f = pending.pop()
            dst, free = fu_at(n)
            hi = act.do(lambda e: e.activation(dst[:, 0, :], f, ACT.Copy), t_f[n], *free)
            lo = dve.do(lambda e: e.tensor_tensor(dst[:, 1, :], f, dst[:, 0, :].bitcast(F32), ALU.subtract), hi)
            ff_free[r] = [hi, lo]
            t_fu[n] = lo

        d_free = [[] for _ in range(NT)]
        t_d = {}

        def d_piece(b, i):
            for t in range(NT):
                d_tile(b, i, t)
            fu_free[i % 2] = [t_d[NT - 1]]

        def d_tile(b, i, t):
            n = b * NI + i
            src = fu_at(n)[0]
            for part in range(2):
                t_d[t] = pe.do(lambda e, part=part: e.matmul(
                    bd[t][:, :], src[:, part, P * t:P * t + P], dw[:, i, :],
                    start=i == 0 and part == 0, stop=i == NI - 1 and part == 1),
                    *([t_fu[n]] + t_dw[i] + (d_free[t] if i == 0 else []) if part == 0 else []), mark=part == 1)

        t_y = {}

        def fin_scale(b, t):
            r = ff_next[0] % 2
            ff_next[0] += 1
            y = ff[:, r, :]
            if b == NB - 1 and t > 1:
                y = sl[:, t - 2, :]
            m = dve.do(lambda e: e.tensor_tensor(y, bd[t][:, :], ds[:, :], ALU.mult), t_d[t], t_sc_load, *(() if b == NB - 1 and t > 1 else ff_free[r]))
            d_free[t] = [m]
            t_y[b, t] = (r, y, m)

        def fin_add(b, t, on):
            r, y, m = t_y[b, t]
            hh = h[:, b % 2, t, :]
            a = on.do(lambda e: e.tensor_tensor(hh, y, hh, ALU.add), m)
            ff_free[r] = [a]
            h_free[b % 2][t:t + 1] = [[dma(out[D * b + P * t:D * b + P * t + P, :], hh, f"o{b % 2}{t}", a)]]

        def fin_piece(b):
            h_free[b % 2] = [[] for _ in range(NT)]
            for t in range(NT):
                fin_scale(b, t)
                fin_add(b, t, pool)

        chunks = []
        for c in range(3):
            for w, src in ((0, gate_w), (1, up_w)):
                for k in range(KT):
                    chunks.append((src[P * k:P * k + P, 512 * c:512 * c + 512], gu[:, c, 4 * w + k, :], c, None))
            for i in range(4 * c, 4 * c + 4):
                chunks.append((down_w[P * i:P * i + P, :], dw[:, i, :], c, i))
        t_gu = {c: [] for c in range(3)}
        t_dw = {}
        st_free = [[] for _ in range(4)]
        t_st = {}
        mq_free = [[], [], []]

        def load_chunk(n):
            t_st[n] = dma(stage[:, n % 4, :], chunks[n][0], f"st{n % 4}", *st_free[n % 4])

        MQ = 3
        e_next, r_next = [0], [0]
        t_e = {}

        def expo(count=1):
            for _ in range(count):
                n = e_next[0]
                if n == len(chunks):
                    return
                assert n < r_next[0] + MQ
                e_next[0] += 1
                m = mq[:, n % MQ, :]
                top = stage[:, n % 4, :].bitcast(U16).rearrange("p (n t) -> p n t", t=2)[:, :, 1]
                x = dve.do(lambda e, m=m, top=top: e.tensor_scalar(m.bitcast(U16), top, 0x7F80, 0x0040,
                                                                   ALU.bitwise_and, ALU.bitwise_or),
                           t_st[n], *mq_free[n % MQ])
                t_e[n] = dve.do(lambda e, m=m: e.tensor_scalar(m, m, 1.5 * 2.0 ** -6, 2.0 ** 20, ALU.max, ALU.mult), x)

        def rnd(*on):
            for eng in on:
                n = r_next[0]
                if n == len(chunks):
                    return
                r_next[0] += 1
                _, dst, c, i = chunks[n]
                w, m = stage[:, n % 4, :], mq[:, n % MQ, :]
                after = wo_raw_read if (i is None and c == 2) else raw_read[1] if (i is None and c == 1) else []
                a = eng.do(lambda e, w=w, m=m: e.tensor_tensor(w, w, m, ALU.add), t_e[n])
                b = eng.do(lambda e, w=w, m=m, dst=dst: e.tensor_tensor(dst, w, m, ALU.subtract), a, *after)
                mq_free[n % MQ] = [b]
                st_free[n % 4] = [b]
                if i is None:
                    t_gu[c].append(b)
                else:
                    t_dw[i] = [b]
                if n + 4 < len(chunks):
                    load_chunk(n + 4)
                else:
                    hT_free[1].append(b)

        t_raw = {}
        for w, src in ((0, w_q), (1, w_kv)):
            for f in range(KT):
                t_raw[w, f] = dma(raw[w][:, f, :], src[P * f:P * f + P, :], f"raw{w}{f}")
                if w == 0 and f == 0:
                    t_cst = dma(cst[:, :], cst_d, "cst")
        for k in range(KT):
            load_xT(0, k)
        load_chunk(0)
        load_chunk(1)
        t_cst2 = dma(cst2, cst2_d, "cst2")
        load_x(0)
        load_chunk(2)
        load_chunk(3)
        t_woR = dma(woR, woT.rearrange("(f p) n -> p f n", p=P), "woR")
        load_xT(1, 0)
        load_xT(1, 1)
        dma(gs[:, :], gs_d, "sc")
        dma(us[:, :], us_d, "sc")
        t_sc_load = dma(ds[:, :], ds_d.rearrange("(a n) -> a n", a=1).broadcast_to([P, D]), "sc")

        t_wf = {}
        raw_read = [[], []]
        wo_raw_read = []

        def center():
            st, ag, out = {}, {}, ([], [])

            def stats(j):
                st[j] = dve.do(lambda e: e.bn_stats(wst[:, j, :], raw[j // KT][:, j % KT, :]), t_raw[j // KT, j % KT])

            def aggr(j):
                ag[j] = dve.do(lambda e: e.bn_aggr(wmv[:, j, :], wst[:, j, :]), st[j])

            def less(j):
                rows = raw[j // KT][:, j % KT, :]
                if j < KT:
                    ng = dve.do(lambda e: e.tensor_scalar(wmv[:, j, 1:2], wmv[:, j, 0:1], -1.0, None, ALU.mult), ag[j])
                    out[0].append(act.do(lambda e: e.activation(rows, rows, ACT.Identity, bias=wmv[:, j, 1:2]), ng))
                else:
                    out[1].append(dve.do(lambda e: e.tensor_scalar(rows, rows, wmv[:, j, 0:1], None, ALU.subtract), ag[j]))

            stats(0)
            aggr(0)
            less(0)
            stats(1)
            aggr(1)
            for j in range(2, 2 * KT):
                stats(j)
                less(j - 1)
                aggr(j)
            less(2 * KT - 1)
            return out

        def transform(w, t_c):
            at = [a_bank() for _ in range(KT)]
            done = {}
            for f in range(KT):
                for k, i in enumerate(at):
                    done[k] = pe.do(lambda e, f=f, i=i, k=k: e.matmul(
                        ba[i][:, P * f:P * f + P], raw[w][:, f, P * k:P * k + P], fwd, start=True, stop=True),
                        *(a_free[i] + [t_cst] if f == 0 else []), *([t_c[f]] if k == 0 else []), mark=f == KT - 1)
            raw_read[w] = [done[KT - 1]]
            return at, done

        def split_wf(w, at, done):
            for k, i in enumerate(at):
                hi = act.do(lambda e, i=i, k=k: e.activation(wf[:, w, 0, k, :], ba[i][:, :], ACT.Copy), done[k])
                lo = dve.do(lambda e, i=i, k=k: e.tensor_tensor(wf[:, w, 1, k, :], ba[i][:, :],
                                                                wf[:, w, 0, k, :].bitcast(F32), ALU.subtract), hi)
                a_free[i] = [lo]
                t_wf[w, k] = lo

        t_wo = []

        wo_at, wo_hi, wo_mi = {}, {}, {}

        def wo_high(j):
            i = wo_at[j] = a_bank()
            m = pe.do(lambda e: e.matmul(ba[i][:, :], inv, woR[:, j, :], start=True, stop=True), *a_free[i], t_woR, t_cst2)
            wo_raw_read[:] = [m]
            wo_hi[j] = act.do(lambda e: e.activation(wo[:, 0, j, :], ba[i][:, :], ACT.Copy), m)

        def wo_low_mm(j):
            i = wo_at[j]
            wo_mi[j] = pe.do(lambda e: e.matmul(ba[i][:, :], minus[:, :], wo[:, 0, j, :], start=False, stop=True,
                                                skip_group_check=True), wo_hi[j])

        def wo_low(j):
            i = wo_at[j]
            lo = act.do(lambda e: e.activation(wo[:, 1, j, :], ba[i][:, :], ACT.Copy), wo_mi[j])
            a_free[i] = [lo]
            t_wo[:] = [lo]

        one = dve.do(lambda e: e.memset(Q[:, 0, 0:1], 1.0))
        act.do(lambda e: e.activation(Q[:, 0, 1:2], Q[:, 0, 0:1], ACT.Sqrt), one)
        t_c0, t_c1 = center()
        wf0 = transform(0, t_c0)
        split_xT(0, 0)
        split_xT(0, 1)
        split_xT(0, 2, dve)
        split_xT(0, 3, dve)
        split_wf(0, *wf0)
        wf1 = transform(1, t_c1)
        spare(0, "a0")
        split_wf(1, *wf1)
        hT_free[0] = raw_read[0]
        spare(0, "a1")
        qk_mm(0, 0, 0)
        qk_mm(0, 0, 1)
        qk_sum(0, 0, 0)
        qk_sum(0, 0, 1)
        act.do(lambda e: e.activation(minus[:, :], ident, ACT.Copy, scale=-1.0), t_cst)
        t_tr16 = act.do(lambda e: e.activation(tr16[:, :, :], cst2[:, 128:384].rearrange("p (a n) -> p a n", a=2), ACT.Copy),
                        t_cst2)
        qk_mm(0, 1, 0)
        qk_mm(0, 1, 1)
        for t in range(NT):
            stats1(0, t)
        spare(0, "a2")
        qk_sum(0, 1, 0)
        qk_sum(0, 1, 1)
        norm_piece(0, [0, 1], lambda: spare(0, "a3"))
        spare(0, "a4")
        qk_mm(0, 2, 0)
        qk_mm(0, 2, 1)
        scale_kv(0, 0)
        scale_kv(0, 1)
        qk_sum(0, 2, 0)
        qk_sum(0, 2, 1)
        qk_mm(0, 3, 0)
        qk_mm(0, 3, 1)
        scale_q(0, 0)
        scale_q(0, 1)
        spare(0, "a5")
        qk_sum(0, 3, 0)
        tri_mm(0, 0)
        tri_mm(0, 1)
        product(0, 0)
        spare(0, "p0")
        qk_sum(0, 3, 1)
        wo_high(0)
        norm_piece(0, [2, 3])
        for j in range(1, KT):
            wo_high(j)
        scale_kv(0, 2)
        scale_kv(0, 3)
        product(0, 1)
        for j in range(KT):
            wo_low_mm(j)
        pt_piece(0, 0)
        for j in range(KT):
            wo_low(j)
        scale_q(0, 2)
        scale_q(0, 3)
        load_x(1)
        tri_mm(0, 2)
        product(0, 2)
        spare(0, "p1")
        tri_mm(0, 3)
        product(0, 3)
        pt_piece(0, 1)
        spare(0, "p2")
        o_piece(0, 0)
        pt_piece(0, 2)
        spare(0, "p3")
        split_xT(1, 0)
        split_xT(1, 1)
        spare(0, "p4")
        load_xT(1, 2)
        load_xT(1, 3)
        o_piece(0, 1)
        pt_piece(0, 3)
        ln2_piece(0, [0, 1])
        split_xT(1, 2)
        split_xT(1, 3)
        spare(0, "p5")
        hn_piece(0, 0)
        hn_piece(0, 1)
        spare(0, "p6")
        o_piece(0, 2)
        o_piece(0, 3)
        spare(0, "p7")
        ln2_piece(0, [2, 3])
        hn_piece(0, 2)
        hn_piece(0, 3)
        spare(0, "p8")
        ht_piece(0, 0)
        ht_piece(0, 1)
        spare(0, "p9")
        qk_mm(1, 0, 0)
        ht_piece(0, 2)
        ht_piece(0, 3)
        spare(0, "p10")
        qk_mm(1, 0, 1)
        qk_sum(1, 0, 0)
        spare(0, "p11")
        qk_sum(1, 0, 1)
        spare(0, "p12")

        a_banks[0] = 2
        pT_bufs[0] = 1
        fu_free[:] = pT_free[1:]
        g_free, u_free = a_free[2], a_free[3]
        for t in range(NT):
            d_free[t] = a_free[4 + t]
            ff_free[t % 2] = tu_free[0]
        def before_d(b, slot):
            if slot in (0, 1) and (b, slot) != (1, 0):
                qk_piece(b, slot)
            if slot == 2:
                qk_piece(b, 3)
            if 6 <= slot <= 9:
                o_piece(b, slot - 6)
            if 5 <= slot <= 8:
                pt_piece(b, slot - 5)
            if slot == 3:
                scale_kv(b, 0)
                spare(b - 1, "kv0")
            if slot == 4:
                tri_piece(b, 0)
            if slot == 10:
                ht_piece(b, 0)
                ht_piece(b, 1)
            if slot == 11:
                ht_piece(b, 3)

        def behind_d(b, slot):
            if slot == 1:
                qk_piece(b, 2)
                for t in range(NT):
                    stats1(b, t)
                    if t == 1:
                        spare(b - 1, "stats")
            if slot == 2:
                norm_piece(b, range(NT))
            if slot == 3:
                scale_kv(b, 1)
                scale_q(b, 0)
                scale_kv(b, 2)
                scale_kv(b, 3)
            if slot == 4:
                for t in range(1, NT):
                    scale_q(b, t)
            if 5 <= slot <= 7:
                tri_piece(b, slot - 4)
            if slot == 9:
                ln2_piece(b, range(NT))
                for t in range(NT):
                    hn_piece(b, t)
            if slot == 10:
                ht_piece(b, 2)

        for b in range(NB):
            for i in range(NI):
                gu_piece(b, i)
                spare(b, f"gu{i}")
                if b + 1 < NB and 5 <= i <= 7:
                    split_kv(b + 1, i - 4)
                    spare(b, f"kv{i - 4}")
                if b + 1 < NB:
                    before_d(b + 1, i)
                if (b, i) != (0, 0) and b * NI + i < NB * NI - 2:
                    d_piece(*divmod(b * NI + i - 1, NI))
                split_f()
                spare(b, f"split{i}")
                if b + 1 < NB:
                    behind_d(b + 1, i)
                spare(b, f"end{i}")
                if i == 0 and b > 0:
                    fin_piece(b - 1)
                    if b + 1 < NB:
                        load_x(b + 1)
                if b + 2 < NB:
                    if i == 4:
                        load_xT(b + 2, 0)
                        load_xT(b + 2, 1)
                    if 6 <= i < 10:
                        split_xT(b + 2, i - 6)
                        if i < 8:
                            load_xT(b + 2, i - 4)

        b = NB - 1
        d_piece(b, NI - 3)
        for t, i in ((0, NI - 2), (1, NI - 2), (0, NI - 1), (2, NI - 2), (1, NI - 1), (3, NI - 2), (2, NI - 1), (3, NI - 1)):
            d_tile(b, i, t)
        h_free[b % 2] = [[] for _ in range(NT)]
        for t in range(NT):
            fin_scale(b, t)
            if t < 2:
                fin_add(b, t, pool)
        fin_add(b, 3, dve)
        fin_add(b, 2, dve)
        for name, s in sent.items():
            if name[0] == "o":
                sp.do(lambda e: e.nop(), (s[0], s[1]), mark=False)

        with nc.Block() as block:
            @block.sync
            def _(e):
                sp.run(e)

            @block.tensor
            def _(e):
                pe.run(e)

            @block.scalar
            def _(e):
                act.run(e)

            @block.vector
            def _(e):
                dve.run(e)

            @block.gpsimd
            def _(e):
                pool.run(e)


def kernel(L0_attn_x, L0_attn_W_q, L0_attn_W_kv, L0_attn_W_o, L0_ffn_gate_w, L0_ffn_up_w, L0_ffn_down_w,
           L0_ffn_gate_scale, L0_ffn_up_scale, L0_ffn_down_scale):
    import concourse.bacc as bacc
    from concourse.bass_utils import run_bass_kernel_spmd

    x = np.ascontiguousarray(np.asarray(L0_attn_x).reshape(NB * D, D))
    cst, cst2 = constants()
    arrays = {
        "x": x,
        "xT": np.ascontiguousarray(x.T),
        "w_q": np.ascontiguousarray(L0_attn_W_q),
        "w_kv": np.ascontiguousarray(L0_attn_W_kv),
        "woT": np.ascontiguousarray(np.asarray(L0_attn_W_o).T),
        "gate_w": np.ascontiguousarray(L0_ffn_gate_w),
        "up_w": np.ascontiguousarray(L0_ffn_up_w),
        "down_w": np.ascontiguousarray(L0_ffn_down_w),
        "gs": np.ascontiguousarray(np.asarray(L0_ffn_gate_scale).reshape(NI, P).T),
        "us": np.ascontiguousarray(np.asarray(L0_ffn_up_scale).reshape(NI, P).T),
        "ds": np.ascontiguousarray(L0_ffn_down_scale),
        "cst": cst,
        "cst2": cst2,
    }
    nc = bacc.Bacc("TRN2", target_bir_lowering=False, num_devices=1)
    args = [nc.dram_tensor(n + "_dram", a.shape, mybir.dt.from_np(a.dtype), kind="ExternalInput").ap()
            for n, a in arrays.items()]
    out = nc.dram_tensor("out_dram", (NB * D, D), F32, kind="ExternalOutput").ap()
    build(nc, *args, out)
    r = run_bass_kernel_spmd(nc, [{n + "_dram": a for n, a in arrays.items()}], core_ids=[0])
    return r.results[0]["out_dram"].reshape(NB, D, D)
```
